# Optimizing a Trainium2 kernel written in Bass

```python
import numpy as np
import jax
import jax.numpy as jnp

def _softmax(x, axis=-1):
    return jax.nn.softmax(x, axis=axis)

def _gelu(x):
    return jax.nn.gelu(x, approximate=True)

def _silu(x):
    return jax.nn.silu(x)

def _sigmoid(x):
    return jax.nn.sigmoid(x)

def _layernorm(x, axis=-1, eps=1e-05):
    m = jnp.mean(x, axis=axis, keepdims=True)
    v = jnp.var(x, axis=axis, keepdims=True)
    return (x - m) / jnp.sqrt(v + eps)

def _scatter_add(tgt, idx, src, axis=0):
    return tgt.at[idx].add(src)

def _segment_sum(src, seg, n):
    return jax.ops.segment_sum(src, seg, n)
kernel_name = 'mk_gnn_resnorm_d1_gnn_r32_179265'

def setup_inputs(seed: int=0):
    np.random.seed(seed)
    _w = jnp.asarray

    def _rec_inputs():
        import jax
        import jax.numpy as jnp
        _gk = jax.random.key(seed)
        x = -0.0003713 + 1 * jax.random.normal(jax.random.fold_in(_gk, 1), (3125, 128), jnp.float32)
        src = jax.random.randint(jax.random.fold_in(_gk, 2), (50000,), 0, 3125, jnp.int32)
        dst = jax.random.randint(jax.random.fold_in(_gk, 3), (50000,), 0, 3125, jnp.int32)
        _o = jnp.argsort(dst, stable=True)
        src = src[_o]
        dst = dst[_o]
        return (x, src, dst)
    x, src, dst = _rec_inputs()

    def _L0_gnn_setup():
        import jax, jax.numpy as jnp
        import numpy as np
        N_NODES = 3125
        N_EDGES = 18750
        H = 128
        NUM_STEPS = 5
        key = jax.random.key(seed)
        ks = jax.random.split(key, 8)
        s = 0.05
        return {'x': jax.random.normal(ks[0], (N_NODES, H), dtype=jnp.float32), 'edge_index': jax.random.randint(ks[1], (2, N_EDGES), 0, N_NODES, dtype=jnp.int64), 'W_msg': jax.random.normal(ks[2], (H, H), dtype=jnp.float32) * s, 'b_msg': jax.random.normal(ks[3], (H,), dtype=jnp.float32) * s, 'W_ih': jax.random.normal(ks[4], (3 * H, H), dtype=jnp.float32) * s, 'W_hh': jax.random.normal(ks[5], (3 * H, H), dtype=jnp.float32) * s, 'b_ih': jax.random.normal(ks[6], (3 * H,), dtype=jnp.float32) * s, 'b_hh': jax.random.normal(ks[7], (3 * H,), dtype=jnp.float32) * s}
    _L0_gnn_all = _L0_gnn_setup()
    _L0_gnn_in = {k: v for k, v in _L0_gnn_all.items() if k in ('W_msg', 'b_msg', 'W_ih', 'W_hh', 'b_ih', 'b_hh')}
    del _L0_gnn_all
    return {'x': x, 'src': src, 'dst': dst, 'L0_gnn_W_msg': _L0_gnn_in['W_msg'], 'L0_gnn_b_msg': _L0_gnn_in['b_msg'], 'L0_gnn_W_ih': _L0_gnn_in['W_ih'], 'L0_gnn_W_hh': _L0_gnn_in['W_hh'], 'L0_gnn_b_ih': _L0_gnn_in['b_ih'], 'L0_gnn_b_hh': _L0_gnn_in['b_hh']}

def reference(x, src, dst, L0_gnn_W_msg, L0_gnn_b_msg, L0_gnn_W_ih, L0_gnn_W_hh, L0_gnn_b_ih, L0_gnn_b_hh):
    import jax
    import jax.numpy as jnp

    def _L0_gnn_ref(x, edge_index, W_msg, b_msg, W_ih, W_hh, b_ih, b_hh):
        import jax, jax.numpy as jnp
        import numpy as np
        N_NODES = 3125
        N_EDGES = 18750
        H = 128
        NUM_STEPS = 5
        num_nodes = x.shape[0]
        row, col = (edge_index[0], edge_index[1])

        def step(h, _):
            messages = h[col] @ W_msg.T + b_msg
            agg = jax.ops.segment_sum(messages, row, num_segments=num_nodes)
            gi = agg @ W_ih.T + b_ih
            gh = h @ W_hh.T + b_hh
            i_r, i_z, i_n = jnp.split(gi, 3, axis=-1)
            h_r, h_z, h_n = jnp.split(gh, 3, axis=-1)
            r = jax.nn.sigmoid(i_r + h_r)
            z = jax.nn.sigmoid(i_z + h_z)
            n = jnp.tanh(i_n + r * h_n)
            h_new = (1.0 - z) * n + z * h
            return (h_new, None)
        h, _ = jax.lax.scan(step, x, None, length=NUM_STEPS)
        return h
    edge_index = jnp.stack([src, dst])
    x = _layernorm(x + _L0_gnn_ref(x, edge_index, L0_gnn_W_msg, L0_gnn_b_msg, L0_gnn_W_ih, L0_gnn_W_hh, L0_gnn_b_ih, L0_gnn_b_hh), axis=-1)
    return x

_drawn_inputs = setup_inputs


def setup_inputs(seed=0):
    import zlib

    import numpy as np

    out = dict(_drawn_inputs(seed))
    spreads = {}
    factors = {}
    for name, (base, spread) in spreads.items():
        noise = np.random.default_rng([zlib.crc32(name.encode()), seed]).standard_normal(out[name].shape)
        drawn = base * np.exp(spread * noise) if base else spread * noise
        out[name] = jnp.asarray(drawn.astype(out[name].dtype))
    for name, factor in factors.items():
        out[name] = (out[name] * factor).astype(out[name].dtype)
    return out
```

```python
from contextlib import ExitStack

import concourse.bass as bass
from concourse import mybir

ALU = mybir.AluOpType
ACT = mybir.ActivationFunctionType
F32 = mybir.dt.float32
F16 = mybir.dt.float16
BF16 = mybir.dt.bfloat16
I32 = mybir.dt.int32

P = 128
H = 128
STEPS = 5
EPS = 1e-5
GROUP = 16
RANGES = P // GROUP
WIN = 384
CHUNKS = WIN // P
BANKS = 8
BANK = 512
RING = 4


def gnn_kernel(nc, x, src, dst, w_msg, b_msg, w_ih, w_hh, b_ih, b_hh, out):
    N = x.shape[0]
    E = src.shape[0]
    KT = -(-N // P)
    GT = P // GROUP
    TAIL = N - (KT - 1) * P
    NG = KT * GT
    SETS = 2
    GS = NG // SETS
    RB = NG * GROUP // RANGES
    NP = RANGES * RB
    DR = 125
    DW = E // DR
    UNITS = -(-KT // 2)
    assert GS * SETS == NG and NP == NG * GROUP and NP >= N and DR * DW == E and (KT - 1) % 2 == 0

    with ExitStack() as ctx:
        def sb(name, shape, dt):
            return ctx.enter_context(nc.sbuf_tensor(name, shape, dt))

        def sem(name):
            return ctx.enter_context(nc.semaphore(name))

        A = sb("A", [P, KT, NP], F16)
        parts = sb("parts", [P, KT, 3, H], BF16)
        hT = sb("hT", [P, NP], F32)
        scratch = sb("scratch", [P, 3840], F32)
        ident = sb("ident", [P, P], F32)
        wT = sb("wT", [P, 7, P], F32)
        bmsg = sb("bmsg", [P, H], F32)
        bih = sb("bih", [P, 3], F32)
        bhh = sb("bhh", [P, 3], F32)
        brz = sb("brz", [P, 2], F32)
        ones = sb("ones", [P, 1], F32)
        small = sb("small", [P, 16], F32)
        smalli = sb("smalli", [P, 8], I32)
        flag = sb("flag", [1, 1], I32)

        PS = ctx.enter_context(nc.psum_tensor("PS", [P, BANKS, BANK], F32))

        def view(t, lo, n, dt=F32):
            size = 2 if dt in (F16, BF16) else 4
            own = 2 if t.dtype in (F16, BF16) else 4
            flat = t[:, lo // own:(lo + n * size) // own]
            return flat if dt == t.dtype else flat.bitcast(dt)

        class Flat:
            def __init__(self, ap, dt):
                self.ap, self.dtype = ap, dt

            def __getitem__(self, k):
                return self.ap[k]

        A_flat = Flat(A[:, :, :].rearrange("p k n -> p (k n)"), F16)
        parts_flat = Flat(parts[:, :, :, :].rearrange("p k t h -> p (k t h)"), BF16)
        s_flat = Flat(scratch[:, :], F32)

        at = [(KT - 5) * NP * 2]

        def prep(n, dt):
            v = view(A_flat, at[0], n, dt)
            at[0] += n * 4
            return v

        dst_rows = prep(DW, I32)
        below = prep(NG, F32)
        thr_row = prep(NG, F32)
        row_of = prep(SETS * DW, I32).rearrange("p (s w) -> p s w", s=SETS)
        win_dst = prep(SETS * WIN, I32).rearrange("p (s w) -> p s w", s=SETS)
        win_src = prep(SETS * WIN, I32).rearrange("p (s w) -> p s w", s=SETS)
        key = prep(SETS * WIN, F32).rearrange("p (s w) -> p s w", s=SETS)
        valid = prep(SETS * WIN, F32).rearrange("p (s w) -> p s w", s=SETS)
        rng = prep(SETS * WIN, F32).rearrange("p (s w) -> p s w", s=SETS)
        rowin = prep(SETS * WIN, F32).rearrange("p (s w) -> p s w", s=SETS)
        place_c, place_q = prep(WIN, I32), prep(WIN, I32)
        assert at[0] <= KT * NP * 2
        x_nodes = view(parts_flat, 0, KT * H, F32).rearrange("p (k h) -> p k h", k=KT)
        w_raw = view(s_flat, 0, 7 * P, F32).rearrange("p (g h) -> p g h", g=7)
        hot = view(parts_flat, 0, RING * CHUNKS * (P + RB), F16).rearrange(
            "p (r c w) -> p r c w", r=RING, c=CHUNKS)
        keyT = view(parts_flat, KT * H * 4, NG * CHUNKS, F32)
        rowT = view(parts_flat, KT * H * 4 + NG * CHUNKS * 4, NG * CHUNKS, F32)
        stage = view(s_flat, 0, 2 * GT * RB, F16).rearrange("p (s q r) -> p s q r", s=2, q=GT)
        iota_row = view(s_flat, 2 * GT * RB * 2, RB, F16)
        iota_key = view(s_flat, 2 * GT * RB * 2 + RB * 2, P, F16)
        at2 = [0]

        def work(n):
            v = view(s_flat, at2[0], n, F32)
            at2[0] += 4 * n
            return v

        agg = [work(RB) for _ in range(2)]
        gate_r, gate_z, pre_n, cand, diff = (work(RB) for _ in range(5))
        msg32 = [work(2 * H).rearrange("p (k h) -> p k h", k=2) for _ in range(2)]
        rest = [work(2 * H).rearrange("p (k h) -> p k h", k=2) for _ in range(2)]
        assert at2[0] <= 3840 * 4
        y = view(A_flat, 0, KT * H, F32).rearrange("p (k h) -> p k h", k=KT)
        stats = view(A_flat, KT * H * 4, KT * 6, F32).rearrange("p (k s) -> p k s", k=KT)
        mv = view(A_flat, KT * H * 4 + 1024, KT * 2, F32).rearrange("p (k s) -> p k s", k=KT)
        std = view(A_flat, KT * H * 4 + 2048, KT, F32)
        rstd = view(A_flat, KT * H * 4 + 3072, KT, F32)
        res = view(A_flat, KT * H * 4 + 4096, KT * H, F32).rearrange("p (k h) -> p k h", k=KT)

        at3 = [20 * 1024 * 2]

        def gen(n, dt=F32):
            v = view(A_flat, at3[0], n, dt)
            at3[0] += 4 * n
            return v

        g_msg = gen(KT * H).rearrange("p (k h) -> p k h", k=KT)
        g_agg, g_iota, g_hot = gen(NP), gen(NP), gen(NP)
        g_src, g_c, g_q = gen(DW, I32), gen(DW, I32), gen(DW, I32)
        g_row, g_edge, g_zero = gen(DW), gen(H), gen(P)
        g_index, g_idle = gen(1, I32), gen(2)
        assert KT * H * 8 + 4096 <= 20 * 1024 * 2 and at3[0] <= (KT - 5) * NP * 2

        thr_part = small[0:GS, 0:2]
        row_f = small[0:GS, 2:4]
        before = small[0:GS, 4:6]
        matched = small[0:GS, 6:8]
        start_f = small[0:GS, 8:10]
        first_dst = small[0:DR, 10:11]
        eps = small[:, 11:12]
        row_i = smalli[0:GS, 0:2]
        start_i = smalli[0:GS, 2:4]

        dst_in, x_in, w_in, b_in = (sem(n) for n in ("dst_in", "x_in", "w_in", "b_in"))
        tail_zeroed, zeroed, consts_made = sem("tail_zeroed"), sem("zeroed"), sem("consts_made")
        prep_chain = sem("prep_chain")
        below_made, rows_counted, rows_set, rows_in = (sem(n) for n in ("below_made", "rows_counted", "rows_set", "rows_in"))
        starts_set, windows_in = sem("starts_set"), [sem("windows_in0"), sem("windows_in1")]
        keys_made, keys_turned, matched_made, matched_summed, flag_set = (
            sem(n) for n in ("keys_made", "keys_turned", "matched_made", "matched_summed", "flag_set"))
        w_turned, w_kept, x_turned, x_kept = (sem(n) for n in ("w_turned", "w_kept", "x_turned", "x_kept"))
        hots_ready, counted, count_kept = sem("hots_ready"), sem("counted"), sem("count_kept")
        stored = [sem("stored0"), sem("stored1")]
        h_ready, msg_made, msg32_ready, part1_done, rest_done, part2_done, parts_ready = (
            sem(n) for n in ("h_ready", "msg_made", "msg32_ready", "part1_done", "rest_done", "part2_done", "parts_ready"))
        agg_made, agg_kept, rz_made, n_made, rz_ready, n_half, pre_ready, cand_ready, d_made, zd_made = (
            sem(n) for n in ("agg_made", "agg_kept", "rz_made", "n_made", "rz_ready", "n_half", "pre_ready",
                             "cand_ready", "d_made", "zd_made"))
        mains_over, y_zeroed, x2_in, out_turned, y_made, stats_made, mv_made, std_made, rstd_made, res_made, out_stored = (
            sem(n) for n in ("mains_over", "y_zeroed", "x2_in", "out_turned", "y_made", "stats_made", "mv_made", "std_made",
                             "rstd_made", "res_made", "out_stored"))

        gs_src_in, gs_idle, gs_consts, gs_rows, gs_msg_made, gs_msg_kept, gs_msg_stored = (
            sem(n) for n in ("gs_src_in", "gs_idle", "gs_consts", "gs_rows", "gs_msg_made", "gs_msg_kept", "gs_msg_stored"))
        gs_index, gs_edges_in, gs_hot, gs_used, gs_summed, gs_agg_kept = (
            sem(n) for n in ("gs_index", "gs_edges_in", "gs_hot", "gs_used", "gs_summed", "gs_agg_kept"))
        gs_gates_made, gs_rz_ready, gs_half, gs_pre_ready, gs_cand_ready, gs_d_made, gs_zd_made = (
            sem(n) for n in ("gs_gates_made", "gs_rz_ready", "gs_half", "gs_pre_ready", "gs_cand_ready", "gs_d_made",
                             "gs_zd_made"))
        messages = nc.dram_tensor("messages", (N, H), F32, kind="Internal").ap()
        MU = -(-KT // 4)

        def by_place(nodes, tiles):
            whole = nodes[0:(KT - 1) * P, :].rearrange("(k q c) h -> q c k h", q=GT, c=GROUP)
            pairs = [(whole[q], tiles[q:P:GT, 0:KT - 1, :]) for q in range(GT)]
            for q in range(-(-TAIL // GROUP)):
                n = min(GROUP, TAIL - q * GROUP)
                first = (KT - 1) * P + q * GROUP
                pairs.append((nodes[first:first + n, :], tiles[q:q + GT * (n - 1) + 1:GT, KT - 1, :]))
            return pairs

        dst_2d = dst.rearrange("(a b) -> a b", b=DW)
        src_2d = src.rearrange("(a b) -> a b", b=DW)

        MOVES = GT + -(-TAIL // GROUP)

        block = ctx.enter_context(nc.Block())

        @block.sync
        def _(sp):
            sp.dma_start(dst_rows[0:DR, :], dst_2d).then_inc(dst_in, 16)
            sp.wait_ge(tail_zeroed, 1)
            for nodes, places in by_place(x, x_nodes):
                sp.dma_start(places, nodes).then_inc(x_in, 16)
            sp.wait_ge(flag_set, 1)
            fast = sp.value_load(flag[0:1, 0:1], min_val=0, max_val=1)
            with sp.If(fast == 1):
                with sp.Fori(0, (KT - 1) // 2) as i:
                    for s in range(2):
                        sp.wait_ge(count_kept, i * (2 * GT) + (GT * (s + 1) + RING))
                        for r in range(RANGES):
                            sp.dma_start(
                                A[:, bass.ds(i * 2 + s, 1), r * RB:(r + 1) * RB].rearrange("p k n -> p (k n)"),
                                stage[r * GROUP:(r + 1) * GROUP, s, :, :]).then_inc(stored[s], 16)
                sp.wait_ge(count_kept, NG + RING)
                for r in range(RANGES):
                    sp.dma_start(A[:, KT - 1, r * RB:(r + 1) * RB],
                                 stage[r * GROUP:(r + 1) * GROUP, 0, :, :]).then_inc(stored[0], 16)
            with sp.Else():
                sp.dma_start(g_src[0:DR, :], src_2d).then_inc(gs_src_in, 16)
                with sp.Fori(0, STEPS) as t:
                    sp.wait_ge(gs_msg_kept, t * MU + (MU + 1))
                    for nodes, places in by_place(messages, g_msg):
                        sp.dma_start(nodes, places).then_inc(gs_msg_stored, 16)
                sp.wait_ge(gs_msg_stored, 16 * MOVES * STEPS + 16)
            sp.wait_ge(mains_over, 1)
            sp.wait_ge(y_zeroed, 1)
            for nodes, places in by_place(x, y):
                sp.dma_start(places, nodes).then_inc(x2_in, 16)
            sp.wait_ge(res_made, KT)
            for nodes, places in by_place(out, res):
                sp.dma_start(nodes, places).then_inc(out_stored, 16)
            sp.wait_ge(out_stored, 16 * MOVES)

        @block.gpsimd
        def _(pool):
            nc.gpsimd.memset(x_nodes[:, KT - 1, :], 0.0).then_inc(tail_zeroed, 1)
            nc.gpsimd.iota(thr_row[0:DR, :], pattern=[[GROUP, NG]], base=0, channel_multiplier=0,
                           allow_small_or_imprecise_dtypes=True)
            nc.gpsimd.iota(thr_part, pattern=[[GROUP * GS, SETS]], base=0, channel_multiplier=GROUP,
                           allow_small_or_imprecise_dtypes=True)
            nc.gpsimd.memset(ones[:, :], 1.0).then_inc(consts_made, 1)
            nc.gpsimd.memset(ident[:, :], 0.0).then_inc(zeroed, 1)
            pool.wait_ge(zeroed, 1)
            nc.gpsimd.affine_select(out=ident[:, :], in_=ident[:, :], compare_op=ALU.not_equal, fill=1.0,
                                    base=0, pattern=[[-1, P]], channel_multiplier=1).then_inc(consts_made, 1)
            nc.gpsimd.iota(iota_row, pattern=[[1, RB]], base=0, channel_multiplier=0,
                           allow_small_or_imprecise_dtypes=True)
            nc.gpsimd.iota(iota_key, pattern=[[1, P]], base=1, channel_multiplier=0,
                           allow_small_or_imprecise_dtypes=True)
            nc.gpsimd.memset(eps, EPS).then_inc(consts_made, 1)
            pool.wait_ge(rows_set, 1)
            for s in range(SETS):
                nc.gpsimd.indirect_dma_start(
                    out=row_of[0:GS, s, :], out_offset=None, in_=dst_2d,
                    in_offset=bass.IndirectOffsetOnAxis(ap=row_i[:, s:s + 1], axis=0)).then_inc(rows_in, 16)
            pool.wait_ge(starts_set, 1)
            for s in range(SETS):
                for data, to in ((dst_2d, win_dst), (src_2d, win_src)):
                    nc.gpsimd.indirect_dma_start(
                        out=to[0:GS, s, :], out_offset=None, in_=data,
                        in_offset=bass.IndirectOffsetOnAxis(ap=start_i[:, s:s + 1], axis=1)).then_inc(windows_in[s], 16)
            pool.wait_ge(flag_set, 1)
            fast = pool.value_load(flag[0:1, 0:1], min_val=0, max_val=1)
            with pool.If(fast == 1):
                with pool.Fori(0, STEPS) as t:
                    for u in range(UNITS):
                        k = 2 * u
                        n, w = P, min(2, KT - k)
                        pool.wait_ge(part2_done, t * UNITS + (u + 1))
                        nc.gpsimd.tensor_tensor(parts[0:n, k:k + w, 2, :], rest[u % 2][0:n, 0:w, :],
                                                parts[0:n, k:k + w, 1, :], ALU.subtract).then_inc(parts_ready, 1)
            with pool.Else():
                nc.gpsimd.iota(g_iota, pattern=[[1, NP]], base=0, channel_multiplier=0,
                               allow_small_or_imprecise_dtypes=True)
                nc.gpsimd.memset(g_zero, 0.0).then_inc(gs_consts, 1)

                def hold_wait(n):
                    pool.wait_ge(gs_idle, n)
                    nc.gpsimd.tensor_tensor(g_idle[:, 1:2], g_idle[:, 0:1], g_idle[:, 0:1], ALU.add).then_inc(gs_idle, 1)

                nc.gpsimd.memset(g_idle[:, 0:1], 0.0).then_inc(gs_idle, 1)
                with pool.Fori(0, STEPS) as t:
                    pool.wait_ge(gs_msg_stored, t * (16 * MOVES) + (16 * MOVES + 16))
                    hold_wait(t * (DW + 1) + 1)
                    with pool.Fori(0, DW) as e:
                        pool.wait_ge(gs_index, t * DW + (e + 1))
                        hold_wait(t * (DW + 1) + (e + 2))
                        nc.gpsimd.indirect_dma_start(
                            out=g_edge[0:DR, :], out_offset=None, in_=messages,
                            in_offset=bass.IndirectOffsetOnAxis(ap=g_index[0:DR, :], axis=0)).then_inc(gs_edges_in, 16)
                pool.wait_ge(gs_edges_in, 16 * DW * STEPS)
            pool.wait_ge(mains_over, 1)
            nc.gpsimd.memset(y[:, KT - 1, :], 0.0).then_inc(y_zeroed, 1)

        @block.tensor
        def _(pe):
            pe.wait_ge(consts_made, 3)
            pe.wait_ge(w_in, 48)
            for g in range(7):
                mm = pe.transpose(PS[:, 6 + g // 4, (g % 4) * P:(g % 4 + 1) * P], w_raw[:, g, :], ident[:, :])
            mm.then_inc(w_turned, 1)
            pe.wait_ge(below_made, 1)
            for s in range(SETS):
                mm = pe.matmul(PS[0:GS, 0, s:s + 1], below[0:DR, s * GS:(s + 1) * GS], ones[0:DR, :],
                               start=True, stop=True)
            mm.then_inc(rows_counted, 1)
            pe.wait_ge(x_in, 16 * MOVES)
            for k in range(KT):
                b = k // 4
                if k % 4 == 0:
                    if b >= 2:
                        pe.wait_ge(x_kept, b - 1)
                mm = pe.transpose(PS[:, 5 if b % 2 else 1, (k % 4) * P:(k % 4 + 1) * P], x_nodes[:, k, :], ident[:, :])
                if k % 4 == 3 or k == KT - 1:
                    mm.then_inc(x_turned, 1)
            pe.wait_ge(x_kept, -(-KT // 4))
            for s in range(SETS):
                pe.wait_ge(keys_made, s + 1)
                for a, t in enumerate((key, rowin)):
                    for c in range(CHUNKS):
                        mm = pe.transpose(PS[:, 1 + 2 * s + a, c * GS:(c + 1) * GS],
                                          t[0:GS, s, c * P:(c + 1) * P], ident[0:GS, 0:GS])
                mm.then_inc(keys_turned, 1)
            pe.wait_ge(matched_made, 1)
            for s in range(SETS):
                mm = pe.matmul(PS[0:1, 0, 8:9], matched[:, s:s + 1], ones[0:GS, :], start=(s == 0), stop=(s == 1))
            mm.then_inc(matched_summed, 1)
            pe.wait_ge(w_kept, 1)
            pe.wait_ge(flag_set, 1)
            fast = pe.value_load(flag[0:1, 0:1], min_val=0, max_val=1)
            with pe.If(fast == 1):
                def count(g, q):
                    pe.wait_ge(hots_ready, g + (q + 1))
                    pe.wait_ge(count_kept, g + (q + 1))
                    for c in range(CHUNKS):
                        mm = pe.matmul(PS[:, q % RING, 0:RB], hot[:, q % RING, c, 0:P], hot[:, q % RING, c, P:P + RB],
                                       start=(c == 0), stop=(c == CHUNKS - 1))
                    mm.then_inc(counted, 1)

                pe.sem_inc(counted, RING)
                with pe.Fori(0, (KT - 1) // 2) as i:
                    for q in range(2 * GT):
                        count(i * (2 * GT), q)
                for q in range(GT):
                    count((KT - 1) * GT, q)

                def gates(t, b):
                    hb = hT[:, b * RB:(b + 1) * RB]
                    gb = agg[b % 2]
                    pe.wait_ge(agg_kept, t * RANGES + (b + 1 + 2))
                    pe.wait_ge(rz_ready, t * RANGES + (b + 1))
                    for g in range(2):
                        pe.matmul(PS[:, 2 + g, 0:RB], wT[:, 3 + g, :], hb, start=True, stop=False)
                        mm = pe.matmul(PS[:, 2 + g, 0:RB], wT[:, g, :], gb, start=False, stop=True)
                    mm.then_inc(rz_made, 1)
                    pe.wait_ge(pre_ready, t * RANGES + (b + 1))
                    pe.matmul(PS[:, 4, 0:RB], wT[:, 5, :], hb, start=True, stop=True)
                    pe.matmul(PS[:, 5, 0:RB], wT[:, 2, :], gb, start=True, stop=True).then_inc(n_made, 1)

                pe.wait_ge(stored[0], 16 * RANGES * ((KT - 1) // 2 + 2))
                pe.wait_ge(stored[1], 16 * RANGES * ((KT - 1) // 2 + 1))
                with pe.Fori(0, STEPS) as t:
                    pe.wait_ge(h_ready, t * RANGES + RANGES)
                    for u in range(UNITS):
                        pe.wait_ge(msg32_ready, t * UNITS + (u + 1))
                        for k in range(2 * u, min(2 * u + 2, KT)):
                            mm = pe.matmul(PS[:, 6 + u % 2, (k % 2) * H:(k % 2 + 1) * H], hT[:, k * P:(k + 1) * P], wT[:, 6, :],
                                           start=True, stop=True)
                        mm.then_inc(msg_made, 1)
                    for b in range(RANGES):
                        pe.wait_ge(agg_kept, t * RANGES + (b + 1))
                        for k in range(KT):
                            if b == 0 and k % 2 == 0:
                                pe.wait_ge(parts_ready, t * UNITS + (k // 2 + 1 + 2))
                            if b > 0 and k == KT // 2:
                                gates(t, b - 1)
                            for j in range(3):
                                mm = pe.matmul(PS[:, b % 2, 0:RB], parts[:, k, j, :],
                                               A[:, k, b * RB:(b + 1) * RB],
                                               start=(k == 0 and j == 0), stop=(k == KT - 1 and j == 2))
                        mm.then_inc(agg_made, 1)
                    gates(t, RANGES - 1)
                pe.sem_inc(mains_over, 1)
            with pe.Else():
                pe.wait_ge(gs_consts, 1)
                pe.wait_ge(h_ready, RANGES)
                with pe.Fori(0, STEPS) as t:
                    pe.wait_ge(h_ready, t * RANGES + RANGES)
                    for u in range(MU):
                        pe.wait_ge(gs_msg_kept, t * MU + (u + 1))
                        for k in range(4 * u, min(4 * u + 4, KT)):
                            mm = pe.matmul(PS[:, 0, (k % 4) * H:(k % 4 + 1) * H], hT[:, k * P:(k + 1) * P], wT[:, 6, :],
                                           start=True, stop=True)
                        mm.then_inc(gs_msg_made, 1)
                    pe.wait_ge(gs_msg_kept, t * MU + (MU + 1))
                    for r in range(RANGES):
                        pe.matmul(PS[:, r, 0:RB], g_zero, g_iota[:, 0:RB], start=True, stop=False, skip_group_check=True)
                    with pe.Fori(0, DW) as e:
                        pe.wait_ge(gs_edges_in, t * (16 * DW) + e * 16 + 16)
                        pe.wait_ge(gs_hot, t * DW + (e + 1))
                        for r in range(RANGES):
                            mm = pe.matmul(PS[:, r, 0:RB], g_edge[0:DR, :], g_hot[0:DR, r * RB:(r + 1) * RB],
                                           start=False, stop=False, skip_group_check=True)
                        mm.then_inc(gs_used, 1)
                    for r in range(RANGES):
                        mm = pe.matmul(PS[:, r, 0:RB], g_zero, g_iota[:, 0:RB], start=False, stop=True,
                                       skip_group_check=True)
                    mm.then_inc(gs_summed, 1)
                    pe.wait_ge(gs_agg_kept, t + 1)
                    for b in range(RANGES):
                        hb, gb = hT[:, b * RB:(b + 1) * RB], g_agg[:, b * RB:(b + 1) * RB]
                        pe.wait_ge(h_ready, t * RANGES + (RANGES + b))
                        for g in range(2):
                            pe.matmul(PS[:, 2 + g, 0:RB], wT[:, 3 + g, :], hb, start=True, stop=False)
                            pe.matmul(PS[:, 2 + g, 0:RB], wT[:, g, :], gb, start=False, stop=True)
                        pe.matmul(PS[:, 4, 0:RB], wT[:, 5, :], hb, start=True, stop=True)
                        pe.matmul(PS[:, 5, 0:RB], wT[:, 2, :], gb, start=True, stop=True).then_inc(gs_gates_made, 1)
                pe.sem_inc(mains_over, 1)
            pe.wait_ge(h_ready, RANGES * (STEPS + 1))
            for k in range(KT):
                if k % 4 == 0 and k >= 16:
                    pe.wait_ge(y_made, k // 4 - 3)
                mm = pe.transpose(PS[:, 4 + (k // 4) % 4, (k % 4) * P:(k % 4 + 1) * P], hT[:, k * P:(k + 1) * P],
                                  ident[:, :])
                if k % 4 == 3 or k == KT - 1:
                    mm.then_inc(out_turned, 1)

        @block.scalar
        def _(act):
            act.dma_start(w_raw[:, 0:3, :], w_ih.rearrange("(g p) h -> p g h", p=P)).then_inc(w_in, 16)
            act.dma_start(w_raw[:, 3:6, :], w_hh.rearrange("(g p) h -> p g h", p=P)).then_inc(w_in, 16)
            act.dma_start(w_raw[:, 6, :], w_msg).then_inc(w_in, 16)
            act.dma_start(bmsg[:, :], bass.AP(tensor=b_msg.tensor, offset=b_msg.offset,
                                              ap=[[0, P], [1, H]])).then_inc(b_in, 16)
            with nc.allow_non_contiguous_dma(reason="biases to partitions, 384 numbers each"):
                act.dma_start(bih[:, :], b_ih.rearrange("(g p) -> p g", p=P)).then_inc(b_in, 16)
                act.dma_start(bhh[:, :], b_hh.rearrange("(g p) -> p g", p=P)).then_inc(b_in, 16)
            act.wait_ge(w_turned, 1)
            nc.scalar.activation(wT[:, 0:4, :], PS[:, 6, :].rearrange("p (g h) -> p g h", g=4), ACT.Copy)
            nc.scalar.activation(wT[:, 4:7, :], PS[:, 7, 0:3 * P].rearrange("p (g h) -> p g h", g=3),
                                 ACT.Copy).then_inc(w_kept, 1)
            for b in range(-(-KT // 4)):
                n = min(4 * P, NP - 4 * b * P)
                act.wait_ge(x_turned, b + 1)
                nc.scalar.activation(hT[:, 4 * b * P:4 * b * P + n], PS[:, 5 if b % 2 else 1, 0:n],
                                     ACT.Copy).then_inc(x_kept, 1)
            act.wait_ge(consts_made, 3)
            act.wait_ge(flag_set, 1)
            fast = act.value_load(flag[0:1, 0:1], min_val=0, max_val=1)
            with act.If(fast == 1):
                def keep_count(g, s, q):
                    act.wait_ge(counted, g + (q + 1 + RING))
                    nc.scalar.activation(stage[:, s, q % GT, :], PS[:, q % RING, 0:RB], ACT.Copy).then_inc(count_kept, 1)

                act.sem_inc(count_kept, RING)
                act.sem_inc(stored[0], 16 * RANGES)
                act.sem_inc(stored[1], 16 * RANGES)
                with act.Fori(0, (KT - 1) // 2) as i:
                    for s in range(2):
                        act.wait_ge(stored[s], i * (16 * RANGES) + 16 * RANGES)
                        for q in range(s * GT, (s + 1) * GT):
                            keep_count(i * (2 * GT), s, q)
                act.wait_ge(stored[0], 16 * RANGES * ((KT - 1) // 2 + 1))
                for q in range(GT):
                    keep_count((KT - 1) * GT, 0, q)
                act.wait_ge(stored[0], 16 * RANGES * ((KT - 1) // 2 + 2))
                act.wait_ge(stored[1], 16 * RANGES * ((KT - 1) // 2 + 1))
                act.sem_inc(agg_kept, 2)
                act.sem_inc(rz_ready, 1)
                act.sem_inc(h_ready, RANGES)

                def part(t, u, j):
                    k = 2 * u
                    n, w = P, min(2, KT - k)
                    if j == 0:
                        act.wait_ge(msg32_ready, t * UNITS + (u + 1 + 2))
                        nc.scalar.activation(parts[0:n, k:k + w, 0, :], msg32[u % 2][0:n, 0:w, :],
                                             ACT.Copy).then_inc(part1_done, 1)
                    else:
                        act.wait_ge(rest_done, t * UNITS + (u + 1 + 2))
                        nc.scalar.activation(parts[0:n, k:k + w, 1, :], rest[u % 2][0:n, 0:w, :],
                                             ACT.Copy).then_inc(part2_done, 1)

                with act.Fori(0, STEPS) as t:
                    part(t, 0, 0)
                    for u in range(UNITS):
                        if u + 1 < UNITS:
                            part(t, u + 1, 0)
                        part(t, u, 1)
                    for b in range(RANGES):
                        c = t * RANGES
                        act.wait_ge(agg_made, c + (b + 1))
                        act.wait_ge(n_made, c + (b + 1))
                        nc.scalar.activation(agg[b % 2], PS[:, b % 2, 0:RB], ACT.Copy).then_inc(agg_kept, 1)
                        act.wait_ge(rz_made, c + (b + 1))
                        act.wait_ge(h_ready, c + (RANGES + b))
                        nc.scalar.activation(gate_r, PS[:, 2, 0:RB], ACT.Sigmoid, bias=brz[:, 0:1])
                        nc.scalar.activation(gate_z, PS[:, 3, 0:RB], ACT.Sigmoid, bias=brz[:, 1:2]).then_inc(rz_ready, 1)
                        act.wait_ge(pre_ready, c + (b + 2))
                        nc.scalar.activation(cand, pre_n, ACT.Tanh, bias=bih[:, 2:3]).then_inc(cand_ready, 1)
            with act.Else():
                act.sem_inc(h_ready, RANGES)
                with act.Fori(0, STEPS) as t:
                    act.wait_ge(gs_summed, t + 1)
                    last = nc.scalar.activation(g_agg.rearrange("p (r c) -> p r c", r=RANGES), PS[:, :, 0:RB], ACT.Copy)
                    last.then_inc(gs_agg_kept, 1)
                    for b in range(RANGES):
                        act.wait_ge(gs_gates_made, t * RANGES + (b + 1))
                        nc.scalar.activation(gate_r, PS[:, 2, 0:RB], ACT.Sigmoid, bias=brz[:, 0:1])
                        nc.scalar.activation(gate_z, PS[:, 3, 0:RB], ACT.Sigmoid, bias=brz[:, 1:2]).then_inc(gs_rz_ready, 1)
                        act.wait_ge(gs_pre_ready, t * RANGES + (b + 1))
                        nc.scalar.activation(cand, pre_n, ACT.Tanh, bias=bih[:, 2:3]).then_inc(gs_cand_ready, 1)
            act.wait_ge(mv_made, KT)
            nc.scalar.activation(std[:, :], mv[:, :, 1], ACT.Sqrt, bias=eps).then_inc(std_made, 1)

        @block.vector
        def _(dve):
            order = [0]

            def link(ins):
                order[0] += 1
                ins.then_inc(prep_chain, 1)
                dve.wait_ge(prep_chain, order[0])

            dve.wait_ge(dst_in, 16)
            link(nc.vector.tensor_copy(first_dst, dst_rows[0:DR, 0:1]))
            dve.wait_ge(consts_made, 1)
            nc.vector.tensor_scalar(below[0:DR, :], thr_row[0:DR, :], first_dst, None, ALU.is_gt).then_inc(below_made, 1)
            dve.wait_ge(rows_counted, 1)
            link(nc.vector.tensor_scalar(row_f, PS[0:GS, 0, 0:SETS], -1.0, 0.0, ALU.add, ALU.max))
            nc.vector.tensor_copy(row_i, row_f).then_inc(rows_set, 1)
            dve.wait_ge(b_in, 48)
            nc.vector.tensor_tensor(brz[:, :], bih[:, 0:2], bhh[:, 0:2], ALU.add)
            dve.wait_ge(rows_in, 32)
            for s in range(SETS):
                last = nc.vector.tensor_scalar(key[0:GS, :, :].rearrange("p s w -> p (s w)")[:, 0:DW], row_of[0:GS, s, :],
                                               thr_part[:, s:s + 1], 0.0, ALU.is_lt, ALU.add,
                                               accum_out=before[:, s:s + 1])
                link(last)
            link(nc.vector.scalar_tensor_tensor(out=start_f, in0=row_f, scalar=float(DW), in1=before,
                                                op0=ALU.mult, op1=ALU.add))
            nc.vector.tensor_scalar(start_i, start_f, float(E - WIN), None, ALU.min).then_inc(starts_set, 1)
            for s in range(SETS):
                d, r, k, v, a, w = (t[0:GS, s, :] for t in (win_dst, win_src, key, valid, rng, rowin))
                r2, r3 = place_c[0:GS, :], place_q[0:GS, :]
                dve.wait_ge(windows_in[s], 32)
                link(nc.vector.tensor_scalar(k, d, thr_part[:, s:s + 1], None, ALU.subtract))
                link(nc.vector.tensor_scalar(v, k, 0.0, None, ALU.is_ge))
                link(nc.vector.scalar_tensor_tensor(out=v, in0=k, scalar=float(GROUP), in1=v, op0=ALU.is_lt,
                                                    op1=ALU.mult, accum_out=matched[:, s:s + 1]))
                link(nc.vector.tensor_scalar(r2, r, GROUP - 1, None, ALU.bitwise_and))
                link(nc.vector.tensor_scalar(r3, r, 4, GT - 1, ALU.logical_shift_right, ALU.bitwise_and))
                link(nc.vector.scalar_tensor_tensor(out=w, in0=r2, scalar=float(GT - 1), in1=r, op0=ALU.mult, op1=ALU.add))
                link(nc.vector.scalar_tensor_tensor(out=w, in0=r3, scalar=-float(GROUP - 1), in1=w, op0=ALU.mult,
                                                    op1=ALU.add))
                link(nc.vector.tensor_scalar(a, w, float(RB), None, ALU.is_ge))
                for m in range(2, RANGES):
                    link(nc.vector.scalar_tensor_tensor(out=a, in0=w, scalar=float(m * RB), in1=a,
                                                        op0=ALU.is_ge, op1=ALU.add))
                link(nc.vector.scalar_tensor_tensor(out=w, in0=a, scalar=-float(RB), in1=w, op0=ALU.mult, op1=ALU.add))
                link(nc.vector.scalar_tensor_tensor(out=k, in0=a, scalar=float(GROUP), in1=k, op0=ALU.mult, op1=ALU.add))
                last = nc.vector.scalar_tensor_tensor(out=k, in0=k, scalar=1.0, in1=v, op0=ALU.add, op1=ALU.mult)
                last.then_inc(keys_made, 1)
                dve.wait_ge(keys_made, s + 1)
            nc.vector.tensor_copy(matched, matched).then_inc(matched_made, 1)
            for s in range(SETS):
                dve.wait_ge(keys_turned, s + 1)
                for a, t in enumerate((keyT, rowT)):
                    last = nc.vector.tensor_copy(
                        t[:, s * GS * CHUNKS:(s + 1) * GS * CHUNKS].rearrange("p (g c) -> p c g", c=CHUNKS),
                        PS[:, 1 + 2 * s + a, 0:CHUNKS * GS].rearrange("p (c g) -> p c g", c=CHUNKS))
            link(last)
            dve.wait_ge(matched_summed, 1)
            nc.vector.tensor_scalar(flag[0:1, 0:1], PS[0:1, 0, 8:9], float(E), None, ALU.is_equal).then_inc(flag_set, 1)
            dve.wait_ge(x_kept, -(-KT // 4))
            dve.wait_ge(consts_made, 3)
            dve.wait_ge(flag_set, 1)
            fast = dve.value_load(flag[0:1, 0:1], min_val=0, max_val=1)
            with dve.If(fast == 1):
                def one_hots(g, q):
                    dve.wait_ge(counted, g + (q + 1))
                    for c in range(CHUNKS):
                        o = q * CHUNKS + c
                        col = bass.ds(g * CHUNKS + o, 1)
                        nc.vector.tensor_scalar(hot[:, q % RING, c, 0:P], iota_key, keyT[:, col], None, ALU.is_equal)
                        last = nc.vector.tensor_scalar(hot[:, q % RING, c, P:P + RB], iota_row, rowT[:, col], None,
                                                       ALU.is_equal)
                    last.then_inc(hots_ready, 1)

                with dve.Fori(0, (KT - 1) // 2) as i:
                    for q in range(2 * GT):
                        one_hots(i * (2 * GT), q)
                for q in range(GT):
                    one_hots((KT - 1) * GT, q)
                dve.sem_inc(msg32_ready, 2)
                dve.sem_inc(parts_ready, 2)
                dve.sem_inc(n_made, 2)
                dve.sem_inc(rest_done, 2)
                dve.sem_inc(pre_ready, 1)

                def message(t, u):
                    k = 2 * u
                    n, w = P, min(2, KT - k)
                    dve.wait_ge(msg_made, t * UNITS + (u + 1))
                    dve.wait_ge(rest_done, t * UNITS + (u + 1))
                    nc.vector.tensor_tensor(msg32[u % 2][0:n, 0:w, :],
                                            PS[0:n, 6 + u % 2, 0:w * H].rearrange("p (k h) -> p k h", k=w),
                                            bmsg[0:n, :].unsqueeze(1).to_broadcast([n, w, H]),
                                            ALU.add).then_inc(msg32_ready, 1)

                with dve.Fori(0, STEPS) as t:
                    message(t, 0)
                    for u in range(UNITS):
                        k = 2 * u
                        n, w = P, min(2, KT - k)
                        if u + 1 < UNITS:
                            message(t, u + 1)
                        dve.wait_ge(part1_done, t * UNITS + (u + 1))
                        dve.wait_ge(parts_ready, t * UNITS + (u + 1))
                        nc.vector.tensor_tensor(rest[u % 2][0:n, 0:w, :], msg32[u % 2][0:n, 0:w, :],
                                                parts[0:n, k:k + w, 0, :], ALU.subtract).then_inc(rest_done, 1)
                    for b in range(RANGES):
                        c = t * RANGES
                        hb = hT[:, b * RB:(b + 1) * RB]
                        dve.wait_ge(n_made, c + (b + 1 + 2))
                        dve.wait_ge(rz_ready, c + (b + 2))
                        nc.vector.scalar_tensor_tensor(out=pre_n, in0=PS[:, 4, 0:RB], scalar=bhh[:, 2:3], in1=gate_r,
                                                       op0=ALU.add, op1=ALU.mult).then_inc(n_half, 1)
                        dve.wait_ge(n_half, c + (b + 1))
                        nc.vector.tensor_tensor(pre_n, PS[:, 5, 0:RB], pre_n, ALU.add).then_inc(pre_ready, 1)
                        dve.wait_ge(cand_ready, c + (b + 1))
                        nc.vector.tensor_tensor(diff, hb, cand, ALU.subtract).then_inc(d_made, 1)
                        dve.wait_ge(d_made, c + (b + 1))
                        nc.vector.tensor_tensor(diff, gate_z, diff, ALU.mult).then_inc(zd_made, 1)
                        dve.wait_ge(zd_made, c + (b + 1))
                        nc.vector.tensor_tensor(hb, cand, diff, ALU.add).then_inc(h_ready, 1)
            with dve.Else():
                dve.wait_ge(gs_src_in, 16)
                nc.vector.tensor_scalar(g_c[0:DR, :], g_src[0:DR, :], GROUP - 1, None, ALU.bitwise_and)
                nc.vector.tensor_scalar(g_q[0:DR, :], g_src[0:DR, :], 4, GT - 1, ALU.logical_shift_right,
                                        ALU.bitwise_and).then_inc(gs_rows, 1)
                dve.wait_ge(gs_rows, 1)
                nc.vector.scalar_tensor_tensor(out=g_row[0:DR, :], in0=g_c[0:DR, :], scalar=float(GT - 1),
                                               in1=g_src[0:DR, :], op0=ALU.mult, op1=ALU.add).then_inc(gs_rows, 1)
                dve.wait_ge(gs_rows, 2)
                nc.vector.scalar_tensor_tensor(out=g_row[0:DR, :], in0=g_q[0:DR, :], scalar=-float(GROUP - 1),
                                               in1=g_row[0:DR, :], op0=ALU.mult, op1=ALU.add).then_inc(gs_rows, 1)
                dve.wait_ge(gs_rows, 3)
                dve.wait_ge(gs_consts, 1)
                dve.sem_inc(gs_used, 1)
                dve.sem_inc(gs_msg_kept, 1)
                dve.sem_inc(gs_msg_stored, 16)
                with dve.Fori(0, STEPS) as t:
                    for u in range(MU):
                        w = min(4, KT - 4 * u)
                        dve.wait_ge(gs_msg_made, t * MU + (u + 1))
                        if u == 0:
                            dve.wait_ge(gs_msg_stored, t * (16 * MOVES) + 16)
                        nc.vector.tensor_tensor(g_msg[:, 4 * u:4 * u + w, :],
                                                PS[:, 0, 0:w * H].rearrange("p (k h) -> p k h", k=w),
                                                bmsg[:, :].unsqueeze(1).to_broadcast([P, w, H]),
                                                ALU.add).then_inc(gs_msg_kept, 1)
                    with dve.Fori(0, DW) as e:
                        dve.wait_ge(gs_used, t * DW + (e + 1))
                        nc.vector.tensor_copy(g_index[0:DR, :], dst_rows[0:DR, bass.ds(e, 1)]).then_inc(gs_index, 1)
                        nc.vector.tensor_scalar(g_hot[0:DR, :], g_iota[0:DR, :], g_row[0:DR, bass.ds(e, 1)], None,
                                                ALU.is_equal).then_inc(gs_hot, 1)
                    for b in range(RANGES):
                        c = t * RANGES
                        hb = hT[:, b * RB:(b + 1) * RB]
                        dve.wait_ge(gs_rz_ready, c + (b + 1))
                        nc.vector.scalar_tensor_tensor(out=pre_n, in0=PS[:, 4, 0:RB], scalar=bhh[:, 2:3], in1=gate_r,
                                                       op0=ALU.add, op1=ALU.mult).then_inc(gs_half, 1)
                        dve.wait_ge(gs_half, c + (b + 1))
                        nc.vector.tensor_tensor(pre_n, PS[:, 5, 0:RB], pre_n, ALU.add).then_inc(gs_pre_ready, 1)
                        dve.wait_ge(gs_cand_ready, c + (b + 1))
                        nc.vector.tensor_tensor(diff, hb, cand, ALU.subtract).then_inc(gs_d_made, 1)
                        dve.wait_ge(gs_d_made, c + (b + 1))
                        nc.vector.tensor_tensor(diff, gate_z, diff, ALU.mult).then_inc(gs_zd_made, 1)
                        dve.wait_ge(gs_zd_made, c + (b + 1))
                        nc.vector.tensor_tensor(hb, cand, diff, ALU.add).then_inc(h_ready, 1)
            dve.wait_ge(x2_in, 16 * MOVES)
            for g in range(-(-KT // 4)):
                w = min(4, KT - 4 * g)
                n = P
                dve.wait_ge(out_turned, g + 1)
                nc.vector.tensor_tensor(y[0:n, 4 * g:4 * g + w, :], y[0:n, 4 * g:4 * g + w, :],
                                        PS[0:n, 4 + g % 4, 0:w * P].rearrange("p (k h) -> p k h", k=w),
                                        ALU.add).then_inc(y_made, 1)
                dve.wait_ge(y_made, g + 1)
                for k in range(4 * g, 4 * g + w):
                    nc.vector.bn_stats(stats[0:n, k, :], y[0:n, k, :]).then_inc(stats_made, 1)
            for k in range(KT):
                n = P
                dve.wait_ge(stats_made, k + 1)
                nc.vector.bn_aggr(mv[0:n, k, :], stats[0:n, k, :]).then_inc(mv_made, 1)
            dve.wait_ge(std_made, 1)
            nc.vector.reciprocal(rstd[:, :], std[:, :]).then_inc(rstd_made, 1)
            dve.wait_ge(rstd_made, 1)
            for k in range(KT):
                n = P
                nc.vector.tensor_scalar(res[0:n, k, :], y[0:n, k, :], mv[0:n, k, 0:1], rstd[0:n, k:k + 1],
                                        ALU.subtract, ALU.mult).then_inc(res_made, 1)


_INS = ['x', 'src', 'dst', 'L0_gnn_W_msg', 'L0_gnn_b_msg', 'L0_gnn_W_ih', 'L0_gnn_W_hh', 'L0_gnn_b_ih', 'L0_gnn_b_hh']


def kernel(**inputs):
    import numpy as _np
    import concourse.bacc as _bacc
    from concourse import mybir as _mybir
    from concourse.bass_utils import run_bass_kernel_spmd as _run

    nc = _bacc.Bacc("TRN2", target_bir_lowering=False, num_devices=1)
    arrays, args = {}, []
    for name in _INS:
        a = _np.ascontiguousarray(inputs[name])
        arrays[f"in_{name}"] = a
        args.append(nc.dram_tensor(f"in_{name}", a.shape, _mybir.dt.from_np(a.dtype), kind="ExternalInput").ap())
    args.append(nc.dram_tensor("out", inputs['x'].shape, _mybir.dt.float32, kind="ExternalOutput").ap())
    gnn_kernel(nc, *args)
    r = _run(nc, [arrays], core_ids=[0])
    return r.results[0]["out"]
```

```python
from contextlib import ExitStack

import concourse.bass as bass
from concourse import mybir

ALU = mybir.AluOpType
ACT = mybir.ActivationFunctionType
F32 = mybir.dt.float32
F16 = mybir.dt.float16
BF16 = mybir.dt.bfloat16
I32 = mybir.dt.int32

P = 128
H = 128
STEPS = 5
EPS = 1e-5
GROUP = 16
RANGES = P // GROUP
WIN = 384
CHUNKS = WIN // P
BANKS = 8
BANK = 512
PAIR = 2
LAG = 2
COUNT_BANKS = (6, 7)
RING = 4
R_BANK, Z_BANK, IN_BANK, HN_BANK = 0, 1, 2, 7
AGG_BANKS = (4, 5)
MSG_BANKS = (3, 6)


def gnn_kernel(nc, x, src, dst, w_msg, b_msg, w_ih, w_hh, b_ih, b_hh, out):
    N = x.shape[0]
    E = src.shape[0]
    KT = -(-N // P)
    GT = P // GROUP
    TAIL = N - (KT - 1) * P
    GLAST = -(-TAIL // GROUP)
    KLAST = GLAST * GROUP
    NG = (KT - 1) * GT + GLAST
    SETS = 2
    GS = NG // SETS
    RB = NG * GROUP // RANGES
    NP = RANGES * RB
    DR = 125
    DW = E // DR
    UNITS = -(-KT // 2)
    BLOCKS = NP // BANK
    REST = NP - BLOCKS * BANK
    assert GS * SETS == NG and NP == NG * GROUP and NP >= N and DR * DW == E and REST > 0
    assert (KT - 1) % 2 == 0 and BLOCKS == COUNT_BANKS[0] and GLAST * 2 == GT

    with ExitStack() as ctx:
        def sb(name, shape, dt):
            return ctx.enter_context(nc.sbuf_tensor(name, shape, dt))

        def sem(name):
            return ctx.enter_context(nc.semaphore(name))

        A = sb("A", [P, KT, NP], F16)
        parts = sb("parts", [P, KT, 3, H], BF16)
        hT = sb("hT", [P, NP], F32)
        scratch = sb("scratch", [P, 6656], F32)
        ident = sb("ident", [P, P], F32)
        wT = sb("wT", [P, 7, P], F32)
        bmsg = sb("bmsg", [P, H], F32)
        bih = sb("bih", [P, 3], F32)
        bhh = sb("bhh", [P, 3], F32)
        brz = sb("brz", [P, 2], F32)
        ones = sb("ones", [P, 1], F32)
        small = sb("small", [P, 16], F32)
        smalli = sb("smalli", [P, 8], I32)
        flag = sb("flag", [1, 1], I32)

        PS = ctx.enter_context(nc.psum_tensor("PS", [P, BANKS, BANK], F32))

        def view(t, lo, n, dt=F32):
            size = 2 if dt in (F16, BF16) else 4
            own = 2 if t.dtype in (F16, BF16) else 4
            flat = t[:, lo // own:(lo + n * size) // own]
            return flat if dt == t.dtype else flat.bitcast(dt)

        class Flat:
            def __init__(self, ap, dt):
                self.ap, self.dtype = ap, dt

            def __getitem__(self, k):
                return self.ap[k]

        A_flat = Flat(A[:, :, :].rearrange("p k n -> p (k n)"), F16)
        parts_flat = Flat(parts[:, :, :, :].rearrange("p k t h -> p (k t h)"), BF16)
        s_flat = Flat(scratch[:, :], F32)

        at = [(KT - 5) * NP * 2]

        def prep(n, dt):
            v = view(A_flat, at[0], n, dt)
            at[0] += n * 4
            return v

        dst_rows = prep(DW, I32)
        below = prep(NG, F32)
        thr_row = prep(NG, F32)
        row_of = prep(SETS * DW, I32).rearrange("p (s w) -> p s w", s=SETS)
        win_dst = prep(SETS * WIN, I32).rearrange("p (s w) -> p s w", s=SETS)
        win_src = prep(SETS * WIN, I32).rearrange("p (s w) -> p s w", s=SETS)
        key = prep(SETS * WIN, F32).rearrange("p (s w) -> p s w", s=SETS)
        valid = prep(SETS * WIN, F32).rearrange("p (s w) -> p s w", s=SETS)
        rng = prep(SETS * WIN, F32).rearrange("p (s w) -> p s w", s=SETS)
        rowin = prep(SETS * WIN, F32).rearrange("p (s w) -> p s w", s=SETS)
        place_c, place_q = prep(WIN, I32), prep(WIN, I32)
        assert at[0] <= KT * NP * 2
        x_nodes = view(A_flat, 0, KT * H, F32).rearrange("p (k h) -> p k h", k=KT)
        w_raw = view(A_flat, KT * H * 4, 7 * P, F32).rearrange("p (g h) -> p g h", g=7)
        at1 = [0]

        def counting(n, dt):
            v = view(s_flat, at1[0], n, dt)
            at1[0] += n * (2 if dt == F16 else 4)
            return v

        stage = counting(2 * GT * RB, F16).rearrange("p (s q r) -> p s q r", s=2, q=GT)
        rowT = counting(NG * CHUNKS, F32)
        keyT = counting(NG * CHUNKS, F16)
        iota_row = counting(RB, F16)
        iota_key = counting(P * PAIR * CHUNKS, F16)
        hot_key = counting(2 * P * PAIR * CHUNKS, F16).rearrange("p (s m c) -> p s m c", s=2, m=P)
        hot_row = [v.rearrange("p (c w) -> p c w", c=CHUNKS) for v in (
            counting(CHUNKS * RB, F16), counting(CHUNKS * RB, F16),
            view(A_flat, (KT - 1) * NP * 2, CHUNKS * RB, F16),
            view(A_flat, (KT - 1) * NP * 2 + CHUNKS * RB * 2, CHUNKS * RB, F16))]
        assert at1[0] <= 6656 * 4
        at2 = [0]

        def work(n):
            v = view(s_flat, at2[0], n, F32)
            at2[0] += 4 * n
            return v

        agg = work(NP)
        gate_r, gate_z, pre_n, cand, diff = (work(RB) for _ in range(5))
        msg32 = [work(2 * H).rearrange("p (k h) -> p k h", k=2) for _ in range(2)]
        rest = [work(2 * H).rearrange("p (k h) -> p k h", k=2) for _ in range(2)]
        assert at2[0] <= 6656 * 4
        y = view(A_flat, 0, KT * H, F32).rearrange("p (k h) -> p k h", k=KT)
        stats = view(A_flat, KT * H * 4, KT * 6, F32).rearrange("p (k s) -> p k s", k=KT)
        mv = view(A_flat, KT * H * 4 + 1024, KT * 2, F32).rearrange("p (k s) -> p k s", k=KT)
        std = view(A_flat, KT * H * 4 + 2048, KT, F32)
        rstd = view(A_flat, KT * H * 4 + 3072, KT, F32)
        res = view(A_flat, KT * H * 4 + 4096, KT * H, F32).rearrange("p (k h) -> p k h", k=KT)

        at3 = [20 * 1024 * 2]

        def gen(n, dt=F32):
            v = view(A_flat, at3[0], n, dt)
            at3[0] += 4 * n
            return v

        g_msg = gen(KT * H).rearrange("p (k h) -> p k h", k=KT)
        g_agg, g_iota, g_hot = gen(NP), gen(NP), gen(NP)
        g_src, g_c, g_q = gen(DW, I32), gen(DW, I32), gen(DW, I32)
        g_row, g_last, g_edge, g_zero = gen(DW), gen(DW), gen(H), gen(P)
        g_index, g_idle = gen(1, I32), gen(2)
        assert KT * H * 8 + 4096 <= 20 * 1024 * 2 and at3[0] <= (KT - 5) * NP * 2

        thr_part = small[0:GS, 0:2]
        row_f = small[0:GS, 2:4]
        before = small[0:GS, 4:6]
        matched = small[0:GS, 6:8]
        start_f = small[0:GS, 8:10]
        first_dst = small[0:DR, 10:11]
        eps = small[:, 11:12]
        row_i = smalli[0:GS, 0:2]
        start_i = smalli[0:GS, 2:4]

        dst_in, x_in, w_in, b_in = (sem(n) for n in ("dst_in", "x_in", "w_in", "b_in"))
        tail_zeroed, zeroed, consts_made = sem("tail_zeroed"), sem("zeroed"), sem("consts_made")
        prep_chain = sem("prep_chain")
        below_made, rows_counted, rows_set, rows_in = (sem(n) for n in ("below_made", "rows_counted", "rows_set", "rows_in"))
        starts_set, windows_in = sem("starts_set"), [sem("windows_in0"), sem("windows_in1")]
        keys_made, keys_turned, matched_made, matched_summed, flag_set = (
            sem(n) for n in ("keys_made", "keys_turned", "matched_made", "matched_summed", "flag_set"))
        w_turned, w_kept, x_turned, x_kept = (sem(n) for n in ("w_turned", "w_kept", "x_turned", "x_kept"))
        hots_ready, counted, count_kept = sem("hots_ready"), sem("counted"), sem("count_kept")
        stored = [sem("stored0"), sem("stored1")]
        h_ready, msg_made, msg32_ready, part1_done, rest_done, part2_done, parts_ready = (
            sem(n) for n in ("h_ready", "msg_made", "msg32_ready", "part1_done", "rest_done", "part2_done", "parts_ready"))
        first_made, agg_made, agg_kept, rz_made, n_made, rz_ready, n_half, pre_ready, cand_ready, d_made, zd_made = (
            sem(n) for n in ("first_made", "agg_made", "agg_kept", "rz_made", "n_made", "rz_ready", "n_half", "pre_ready",
                             "cand_ready", "d_made", "zd_made"))
        mains_over, y_zeroed, x2_in, out_turned, y_made, stats_made, mv_made, std_made, rstd_made, res_made, out_stored = (
            sem(n) for n in ("mains_over", "y_zeroed", "x2_in", "out_turned", "y_made", "stats_made", "mv_made", "std_made",
                             "rstd_made", "res_made", "out_stored"))

        gs_src_in, gs_idle, gs_consts, gs_rows, gs_msg_made, gs_msg_kept, gs_msg_stored = (
            sem(n) for n in ("gs_src_in", "gs_idle", "gs_consts", "gs_rows", "gs_msg_made", "gs_msg_kept", "gs_msg_stored"))
        gs_index, gs_edges_in, gs_hot, gs_used, gs_summed, gs_agg_kept = (
            sem(n) for n in ("gs_index", "gs_edges_in", "gs_hot", "gs_used", "gs_summed", "gs_agg_kept"))
        gs_gates_made, gs_rz_ready, gs_half, gs_pre_ready, gs_cand_ready, gs_d_made, gs_zd_made = (
            sem(n) for n in ("gs_gates_made", "gs_rz_ready", "gs_half", "gs_pre_ready", "gs_cand_ready", "gs_d_made",
                             "gs_zd_made"))
        messages = nc.dram_tensor("messages", (N, H), F32, kind="Internal").ap()
        MU = -(-KT // 4)

        def by_place(nodes, tiles):
            whole = nodes[0:(KT - 1) * P, :].rearrange("(k q c) h -> q c k h", q=GT, c=GROUP)
            pairs = [(whole[q], tiles[q:P:GT, 0:KT - 1, :]) for q in range(GT)]
            for q in range(-(-TAIL // GROUP)):
                n = min(GROUP, TAIL - q * GROUP)
                first = (KT - 1) * P + q * GROUP
                pairs.append((nodes[first:first + n, :], tiles[q:q + GLAST * (n - 1) + 1:GLAST, KT - 1, :]))
            return pairs

        dst_2d = dst.rearrange("(a b) -> a b", b=DW)
        src_2d = src.rearrange("(a b) -> a b", b=DW)

        MOVES = GT + -(-TAIL // GROUP)

        def width(u):
            return min(2, KT - 2 * u), (KLAST if 2 * u == KT - 1 else P)

        def units_within(ranges):
            return min(UNITS - 1, ranges * RB // (2 * P))

        SPLIT0 = 3
        EARLY = units_within(RANGES - 2)
        MIDDLE = EARLY // 2
        LATE = units_within(RANGES - 1)

        block = ctx.enter_context(nc.Block())

        @block.sync
        def _(sp):
            sp.dma_start(dst_rows[0:DR, :], dst_2d).then_inc(dst_in, 16)
            sp.wait_ge(tail_zeroed, 1)
            for nodes, places in by_place(x, x_nodes):
                sp.dma_start(places, nodes).then_inc(x_in, 16)
            sp.wait_ge(flag_set, 1)
            fast = sp.value_load(flag[0:1, 0:1], min_val=0, max_val=1)
            with sp.If(fast == 1):
                with sp.Fori(0, (KT - 1) // 2) as i:
                    for s in range(2):
                        sp.wait_ge(count_kept, i * (2 * GT) + (GT * (s + 1) + 2))
                        for r in range(RANGES):
                            sp.dma_start(
                                A[:, bass.ds(i * 2 + s, 1), r * RB:(r + 1) * RB].rearrange("p k n -> p (k n)"),
                                stage[r * GROUP:(r + 1) * GROUP, s, :, :]).then_inc(stored[s], 16)
                sp.wait_ge(count_kept, NG + 2)
                for r in range(RANGES):
                    sp.dma_start(A[0:KLAST, KT - 1, r * RB:(r + 1) * RB],
                                 stage[r * GROUP:(r + 1) * GROUP, 0, 0:GLAST, :]).then_inc(stored[0], 16)
            with sp.Else():
                sp.dma_start(g_src[0:DR, :], src_2d).then_inc(gs_src_in, 16)
                with sp.Fori(0, STEPS) as t:
                    sp.wait_ge(gs_msg_kept, t * MU + (MU + 1))
                    for nodes, places in by_place(messages, g_msg):
                        sp.dma_start(nodes, places).then_inc(gs_msg_stored, 16)
                sp.wait_ge(gs_msg_stored, 16 * MOVES * STEPS + 16)
            sp.wait_ge(mains_over, 1)
            sp.wait_ge(y_zeroed, 1)
            for nodes, places in by_place(x, y):
                sp.dma_start(places, nodes).then_inc(x2_in, 16)
            sp.wait_ge(res_made, KT)
            for nodes, places in by_place(out, res):
                sp.dma_start(nodes, places).then_inc(out_stored, 16)
            sp.wait_ge(out_stored, 16 * MOVES)

        @block.gpsimd
        def _(pool):
            nc.gpsimd.memset(x_nodes[:, KT - 1, :], 0.0).then_inc(tail_zeroed, 1)
            nc.gpsimd.iota(thr_row[0:DR, :], pattern=[[GROUP, NG]], base=0, channel_multiplier=0,
                           allow_small_or_imprecise_dtypes=True)
            nc.gpsimd.iota(thr_part, pattern=[[GROUP * GS, SETS]], base=0, channel_multiplier=GROUP,
                           allow_small_or_imprecise_dtypes=True)
            nc.gpsimd.memset(ones[:, :], 1.0).then_inc(consts_made, 1)
            nc.gpsimd.memset(ident[:, :], 0.0).then_inc(zeroed, 1)
            pool.wait_ge(zeroed, 1)
            nc.gpsimd.affine_select(out=ident[:, :], in_=ident[:, :], compare_op=ALU.not_equal, fill=1.0,
                                    base=0, pattern=[[-1, P]], channel_multiplier=1).then_inc(consts_made, 1)
            nc.gpsimd.iota(iota_row, pattern=[[1, RB]], base=0, channel_multiplier=0,
                           allow_small_or_imprecise_dtypes=True)
            nc.gpsimd.iota(iota_key, pattern=[[1, P], [0, PAIR * CHUNKS]], base=1, channel_multiplier=0,
                           allow_small_or_imprecise_dtypes=True)
            nc.gpsimd.memset(eps, EPS).then_inc(consts_made, 1)
            pool.wait_ge(rows_set, 1)
            for s in range(SETS):
                nc.gpsimd.indirect_dma_start(
                    out=row_of[0:GS, s, :], out_offset=None, in_=dst_2d,
                    in_offset=bass.IndirectOffsetOnAxis(ap=row_i[:, s:s + 1], axis=0)).then_inc(rows_in, 16)
            def third_part(t, u):
                w, n = width(u)
                pool.wait_ge(part2_done, t * UNITS + (u + 1))
                nc.gpsimd.tensor_tensor(parts[0:n, 2 * u:2 * u + w, 2, :], rest[u % 2][0:n, 0:w, :],
                                        parts[0:n, 2 * u:2 * u + w, 1, :], ALU.subtract).then_inc(parts_ready, 1)

            for u in range(SPLIT0):
                third_part(0, u)
            pool.wait_ge(starts_set, 1)
            for s in range(SETS):
                for data, to in ((dst_2d, win_dst), (src_2d, win_src)):
                    nc.gpsimd.indirect_dma_start(
                        out=to[0:GS, s, :], out_offset=None, in_=data,
                        in_offset=bass.IndirectOffsetOnAxis(ap=start_i[:, s:s + 1], axis=1)).then_inc(windows_in[s], 16)
            for u in range(SPLIT0, UNITS):
                third_part(0, u)
            pool.wait_ge(flag_set, 1)
            fast = pool.value_load(flag[0:1, 0:1], min_val=0, max_val=1)
            with pool.If(fast == 1):
                with pool.Fori(1, STEPS) as t:
                    for u in range(UNITS):
                        third_part(t, u)
            with pool.Else():
                nc.gpsimd.iota(g_iota, pattern=[[1, NP]], base=0, channel_multiplier=0,
                               allow_small_or_imprecise_dtypes=True)
                nc.gpsimd.memset(g_zero, 0.0).then_inc(gs_consts, 1)

                def hold_wait(n):
                    pool.wait_ge(gs_idle, n)
                    nc.gpsimd.tensor_tensor(g_idle[:, 1:2], g_idle[:, 0:1], g_idle[:, 0:1], ALU.add).then_inc(gs_idle, 1)

                nc.gpsimd.memset(g_idle[:, 0:1], 0.0).then_inc(gs_idle, 1)
                with pool.Fori(0, STEPS) as t:
                    pool.wait_ge(gs_msg_stored, t * (16 * MOVES) + (16 * MOVES + 16))
                    hold_wait(t * (DW + 1) + 1)
                    with pool.Fori(0, DW) as e:
                        pool.wait_ge(gs_index, t * DW + (e + 1))
                        hold_wait(t * (DW + 1) + (e + 2))
                        nc.gpsimd.indirect_dma_start(
                            out=g_edge[0:DR, :], out_offset=None, in_=messages,
                            in_offset=bass.IndirectOffsetOnAxis(ap=g_index[0:DR, :], axis=0)).then_inc(gs_edges_in, 16)
                pool.wait_ge(gs_edges_in, 16 * DW * STEPS)
            pool.wait_ge(mains_over, 1)
            nc.gpsimd.memset(y[:, KT - 1, :], 0.0).then_inc(y_zeroed, 1)

        @block.tensor
        def _(pe):
            def message(t, u):
                w, n = width(u)
                pe.wait_ge(msg32_ready, t * UNITS + (u + 1))
                for k in range(w):
                    o = (2 * u + k) * P
                    mm = pe.matmul(PS[0:n, MSG_BANKS[u % 2], k * H:(k + 1) * H], hT[:, o:o + n], wT[:, 6, :],
                                   start=True, stop=True)
                mm.then_inc(msg_made, 1)

            pe.wait_ge(consts_made, 1)
            pe.wait_ge(below_made, 1)
            for s in range(SETS):
                mm = pe.matmul(PS[0:GS, 0, s:s + 1], below[0:DR, s * GS:(s + 1) * GS], ones[0:DR, :],
                               start=True, stop=True)
            mm.then_inc(rows_counted, 1)
            pe.wait_ge(consts_made, 3)
            pe.wait_ge(w_in, 48)
            for g in range(7):
                mm = pe.transpose(PS[:, 6 + g // 4, (g % 4) * P:(g % 4 + 1) * P], w_raw[:, g, :], ident[:, :])
            mm.then_inc(w_turned, 1)
            pe.wait_ge(x_in, 16 * MOVES)
            for k in range(KT):
                b = k // 4
                if k % 4 == 0 and b >= 2:
                    pe.wait_ge(x_kept, b - 1)
                n = KLAST if k == KT - 1 else P
                mm = pe.transpose(PS[:, 4 + b % 2, (k % 4) * P:(k % 4) * P + n], x_nodes[0:n, k, :], ident[0:n, 0:n])
                if k % 4 == 3 or k == KT - 1:
                    mm.then_inc(x_turned, 1)
            pe.wait_ge(w_kept, 1)
            pe.wait_ge(x_kept, -(-KT // 4))
            for u in range(UNITS):
                message(0, u)
            for s in range(SETS):
                pe.wait_ge(keys_made, s + 1)
                for a, t in enumerate((key, rowin)):
                    for c in range(CHUNKS):
                        mm = pe.transpose(PS[:, (0, 1, 4, 5)[2 * s + a], c * GS:(c + 1) * GS],
                                          t[0:GS, s, c * P:(c + 1) * P], ident[0:GS, 0:GS])
                mm.then_inc(keys_turned, 1)
            pe.wait_ge(matched_made, 1)
            for s in range(SETS):
                mm = pe.matmul(PS[0:1, 7, 0:1], matched[:, s:s + 1], ones[0:GS, :], start=(s == 0), stop=(s == 1))
            mm.then_inc(matched_summed, 1)
            pe.wait_ge(flag_set, 1)
            fast = pe.value_load(flag[0:1, 0:1], min_val=0, max_val=1)
            with pe.If(fast == 1):
                def count(g, q):
                    pe.wait_ge(hots_ready, g + (q + 1))
                    pe.wait_ge(count_kept, g + (q + 1))
                    for c in range(CHUNKS):
                        mm = pe.matmul(PS[:, COUNT_BANKS[q % 2], 0:RB], hot_key[:, q // PAIR % 2, :, q % PAIR * CHUNKS + c],
                                       hot_row[q % RING][:, c, :], start=(c == 0), stop=(c == CHUNKS - 1))
                    mm.then_inc(counted, 1)

                def first_product(k, blocks, start=False, stop=False, n=P):
                    for j in blocks:
                        lo, hi = j * BANK, min((j + 1) * BANK, NP)
                        for part in range(3):
                            mm = pe.matmul(PS[:, j, 0:hi - lo],
                                           parts[0:n, bass.ds(k, 1), part, :].rearrange("p k h -> p (k h)"),
                                           A[0:n, bass.ds(k, 1), lo:hi].rearrange("p k h -> p (k h)"),
                                           start=start and part == 0, stop=stop and part == 2, skip_group_check=True)
                    return mm

                def counts_and_product(i, product=True, start=False):
                    for s in range(2):
                        for q in range(GT):
                            count(i * (2 * GT), s * GT + q)
                            if product:
                                if q == 0:
                                    pe.wait_ge(stored[s], i * (16 * RANGES) + 16 * RANGES)
                                if q < BLOCKS:
                                    first_product(i * 2 + (s - LAG), (q,), start=start and s == 0)

                pe.wait_ge(parts_ready, UNITS + 2)
                counts_and_product(0, product=False)
                counts_and_product(1, start=True)
                with pe.Fori(2, (KT - 1) // 2) as i:
                    counts_and_product(i)
                for q in range(GLAST):
                    count((KT - 1) * GT, q)
                    if q == 0:
                        pe.wait_ge(stored[0], 16 * RANGES * ((KT - 1) // 2 + 1))
                    if 2 * q < BLOCKS:
                        first_product(KT - 1 - LAG, range(2 * q, 2 * q + 2))
                pe.wait_ge(stored[1], 16 * RANGES * ((KT - 1) // 2 + 1))
                first_product(KT - 2, range(BLOCKS))
                pe.wait_ge(stored[0], 16 * RANGES * ((KT - 1) // 2 + 2))
                for j in range(BLOCKS):
                    first_product(KT - 1, (j,), stop=True, n=KLAST).then_inc(first_made, 1)
                pe.wait_ge(count_kept, NG + 2)
                for k in range(KT):
                    mm = first_product(k, (BLOCKS,), start=k == 0, stop=k == KT - 1, n=KLAST if k == KT - 1 else P)
                mm.then_inc(first_made, 1)

                def gates(t, b):
                    hb = hT[:, b * RB:(b + 1) * RB]
                    gb = agg[:, b * RB:(b + 1) * RB]
                    pe.wait_ge(agg_kept, t * RANGES + (b + 1))
                    pe.wait_ge(rz_ready, t * RANGES + (b + 1))
                    for g, bank in enumerate((R_BANK, Z_BANK)):
                        pe.matmul(PS[:, bank, 0:RB], wT[:, 3 + g, :], hb, start=True, stop=False)
                        mm = pe.matmul(PS[:, bank, 0:RB], wT[:, g, :], gb, start=False, stop=True)
                    mm.then_inc(rz_made, 1)
                    pe.wait_ge(pre_ready, t * RANGES + (b + 1))
                    pe.matmul(PS[:, HN_BANK, 0:RB], wT[:, 5, :], hb, start=True, stop=True)
                    pe.matmul(PS[:, IN_BANK, 0:RB], wT[:, 2, :], gb, start=True, stop=True).then_inc(n_made, 1)

                def messages(t, units, ranges):
                    pe.wait_ge(h_ready, t * RANGES + ranges)
                    for u in units:
                        message(t, u)

                pe.wait_ge(agg_kept, IN_BANK + 1)
                made = 0
                for b in range(RANGES):
                    gates(0, b)
                    if b == RANGES // 2 - 1:
                        pe.wait_ge(agg_kept, RANGES)
                    if b >= RANGES // 2:
                        ready = units_within(b)
                        messages(1, range(made, ready), b)
                        made = ready

                def product(t, b, k):
                    n = KLAST if k == KT - 1 else P
                    for part in range(3):
                        mm = pe.matmul(PS[:, AGG_BANKS[b % 2], 0:RB], parts[0:n, k, part, :],
                                       A[0:n, k, b * RB:(b + 1) * RB],
                                       start=(k == 0 and part == 0), stop=(k == KT - 1 and part == 2))
                    if k == KT - 1:
                        mm.then_inc(agg_made, 1)

                def step(t, last):
                    for b in range(RANGES):
                        for k in range(KT):
                            if b == 0 and k == KT // 2:
                                messages(t, range(LATE, UNITS), RANGES)
                            if b == 0 and k % 2 == 0:
                                pe.wait_ge(parts_ready, t * UNITS + (k // 2 + 1 + 2))
                            if b > 0 and k == KT // 2:
                                gates(t, b - 1)
                            product(t, b, k)
                            if b == RANGES - 1 and not last and k % 2 == 1 and 3 <= k < 2 * EARLY + 3:
                                messages(t + 1, (k // 2 - 1,), RANGES - 2)
                    if not last:
                        messages(t + 1, range(EARLY, LATE), RANGES - 1)
                    gates(t, RANGES - 1)

                with pe.Fori(1, STEPS - 1) as t:
                    step(t, last=False)
                step(STEPS - 1, last=True)
                pe.sem_inc(mains_over, 1)
            with pe.Else():
                pe.wait_ge(gs_consts, 1)
                pe.wait_ge(h_ready, RANGES)
                with pe.Fori(0, STEPS) as t:
                    pe.wait_ge(h_ready, t * RANGES + RANGES)
                    for u in range(MU):
                        pe.wait_ge(gs_msg_kept, t * MU + (u + 1))
                        for k in range(4 * u, min(4 * u + 4, KT)):
                            n = KLAST if k == KT - 1 else P
                            mm = pe.matmul(PS[0:n, 0, (k % 4) * H:(k % 4 + 1) * H], hT[:, k * P:k * P + n], wT[:, 6, :],
                                           start=True, stop=True)
                        mm.then_inc(gs_msg_made, 1)
                    pe.wait_ge(gs_msg_kept, t * MU + (MU + 1))
                    for r in range(RANGES):
                        pe.matmul(PS[:, r, 0:RB], g_zero, g_iota[:, 0:RB], start=True, stop=False, skip_group_check=True)
                    with pe.Fori(0, DW) as e:
                        pe.wait_ge(gs_edges_in, t * (16 * DW) + e * 16 + 16)
                        pe.wait_ge(gs_hot, t * DW + (e + 1))
                        for r in range(RANGES):
                            mm = pe.matmul(PS[:, r, 0:RB], g_edge[0:DR, :], g_hot[0:DR, r * RB:(r + 1) * RB],
                                           start=False, stop=False, skip_group_check=True)
                        mm.then_inc(gs_used, 1)
                    for r in range(RANGES):
                        mm = pe.matmul(PS[:, r, 0:RB], g_zero, g_iota[:, 0:RB], start=False, stop=True,
                                       skip_group_check=True)
                    mm.then_inc(gs_summed, 1)
                    pe.wait_ge(gs_agg_kept, t + 1)
                    for b in range(RANGES):
                        hb, gb = hT[:, b * RB:(b + 1) * RB], g_agg[:, b * RB:(b + 1) * RB]
                        pe.wait_ge(h_ready, t * RANGES + (RANGES + b))
                        for g in range(2):
                            pe.matmul(PS[:, 2 + g, 0:RB], wT[:, 3 + g, :], hb, start=True, stop=False)
                            pe.matmul(PS[:, 2 + g, 0:RB], wT[:, g, :], gb, start=False, stop=True)
                        pe.matmul(PS[:, 4, 0:RB], wT[:, 5, :], hb, start=True, stop=True)
                        pe.matmul(PS[:, 5, 0:RB], wT[:, 2, :], gb, start=True, stop=True).then_inc(gs_gates_made, 1)
                pe.sem_inc(mains_over, 1)
            pe.wait_ge(h_ready, RANGES * (STEPS + 1))
            for k in range(KT):
                if k % 4 == 0 and k >= 16:
                    pe.wait_ge(y_made, k // 4 - 3)
                n = KLAST if k == KT - 1 else P
                mm = pe.transpose(PS[0:n, 4 + (k // 4) % 4, (k % 4) * P:(k % 4 + 1) * P], hT[:, k * P:k * P + n],
                                  ident[:, :])
                if k % 4 == 3 or k == KT - 1:
                    mm.then_inc(out_turned, 1)

        @block.scalar
        def _(act):
            act.dma_start(w_raw[:, 0:3, :], w_ih.rearrange("(g p) h -> p g h", p=P)).then_inc(w_in, 16)
            act.dma_start(w_raw[:, 3:6, :], w_hh.rearrange("(g p) h -> p g h", p=P)).then_inc(w_in, 16)
            act.dma_start(w_raw[:, 6, :], w_msg).then_inc(w_in, 16)
            act.dma_start(bmsg[:, :], bass.AP(tensor=b_msg.tensor, offset=b_msg.offset,
                                              ap=[[0, P], [1, H]])).then_inc(b_in, 16)
            with nc.allow_non_contiguous_dma(reason="biases to partitions, 384 numbers each"):
                act.dma_start(bih[:, :], b_ih.rearrange("(g p) -> p g", p=P)).then_inc(b_in, 16)
                act.dma_start(bhh[:, :], b_hh.rearrange("(g p) -> p g", p=P)).then_inc(b_in, 16)
            act.wait_ge(w_turned, 1)
            nc.scalar.activation(wT[:, 0:4, :], PS[:, 6, :].rearrange("p (g h) -> p g h", g=4), ACT.Copy)
            nc.scalar.activation(wT[:, 4:7, :], PS[:, 7, 0:3 * P].rearrange("p (g h) -> p g h", g=3),
                                 ACT.Copy).then_inc(w_kept, 1)
            for b in range(-(-KT // 4)):
                n = min(4 * P, NP - 4 * b * P)
                act.wait_ge(x_turned, b + 1)
                nc.scalar.activation(hT[:, 4 * b * P:4 * b * P + n], PS[:, 4 + b % 2, 0:n],
                                     ACT.Copy).then_inc(x_kept, 1)

            def part(t, u, j):
                w, n = width(u)
                if j == 0:
                    act.wait_ge(msg32_ready, t * UNITS + (u + 1 + 2))
                    nc.scalar.activation(parts[0:n, 2 * u:2 * u + w, 0, :], msg32[u % 2][0:n, 0:w, :],
                                         ACT.Copy).then_inc(part1_done, 1)
                else:
                    act.wait_ge(rest_done, t * UNITS + (u + 1 + 2))
                    nc.scalar.activation(parts[0:n, 2 * u:2 * u + w, 1, :], rest[u % 2][0:n, 0:w, :],
                                         ACT.Copy).then_inc(part2_done, 1)

            def split(t, units):
                for u in units:
                    if u == units[0]:
                        part(t, u, 0)
                    if u < units[-1]:
                        part(t, u + 1, 0)
                    part(t, u, 1)

            split(0, range(SPLIT0))
            split(0, range(SPLIT0, UNITS))
            act.wait_ge(consts_made, 3)
            act.wait_ge(flag_set, 1)
            fast = act.value_load(flag[0:1, 0:1], min_val=0, max_val=1)
            with act.If(fast == 1):
                def keep_count(g, s, q):
                    act.wait_ge(counted, g + (q + 1 + RING))
                    nc.scalar.activation(stage[:, s, q % GT, :], PS[:, COUNT_BANKS[q % 2], 0:RB], ACT.Copy).then_inc(count_kept, 1)

                act.sem_inc(count_kept, 2)
                act.sem_inc(stored[0], 16 * RANGES)
                act.sem_inc(stored[1], 16 * RANGES)
                with act.Fori(0, (KT - 1) // 2) as i:
                    for s in range(2):
                        act.wait_ge(stored[s], i * (16 * RANGES) + 16 * RANGES)
                        for q in range(s * GT, (s + 1) * GT):
                            keep_count(i * (2 * GT), s, q)
                act.wait_ge(stored[0], 16 * RANGES * ((KT - 1) // 2 + 1))
                for q in range(GLAST):
                    keep_count((KT - 1) * GT, 0, q)
                act.wait_ge(stored[0], 16 * RANGES * ((KT - 1) // 2 + 2))
                act.wait_ge(stored[1], 16 * RANGES * ((KT - 1) // 2 + 1))
                for j in range(BLOCKS + 1):
                    lo, hi = j * BANK, min((j + 1) * BANK, NP)
                    act.wait_ge(first_made, j + 1)
                    nc.scalar.activation(agg[:, lo:hi], PS[:, j, 0:hi - lo],
                                         ACT.Copy).then_inc(agg_kept, 1 if j < BLOCKS else RANGES - BLOCKS)
                act.sem_inc(rz_ready, 1)
                act.sem_inc(h_ready, RANGES)

                def keep_agg(t, b):
                    act.wait_ge(agg_made, (t - 1) * RANGES + (b + 1))
                    nc.scalar.activation(agg[:, b * RB:(b + 1) * RB], PS[:, AGG_BANKS[b % 2], 0:RB],
                                         ACT.Copy).then_inc(agg_kept, 1)

                def gate_functions(t, b):
                    c = t * RANGES
                    act.wait_ge(rz_made, c + (b + 1))
                    act.wait_ge(h_ready, c + (RANGES + b))
                    nc.scalar.activation(gate_r, PS[:, R_BANK, 0:RB], ACT.Sigmoid, bias=brz[:, 0:1])
                    nc.scalar.activation(gate_z, PS[:, Z_BANK, 0:RB], ACT.Sigmoid, bias=brz[:, 1:2]).then_inc(rz_ready, 1)
                    act.wait_ge(pre_ready, c + (b + 2))
                    nc.scalar.activation(cand, pre_n, ACT.Tanh, bias=bih[:, 2:3]).then_inc(cand_ready, 1)

                made = 0
                for b in range(RANGES):
                    gate_functions(0, b)
                    if b >= RANGES // 2:
                        ready = units_within(b)
                        split(1, range(made, ready))
                        made = ready

                def step(t, last):
                    split(t, range(LATE, UNITS))
                    for b in range(RANGES):
                        keep_agg(t, b)
                        if b == RANGES - 1 and not last:
                            split(t + 1, range(EARLY, LATE))
                        if b == RANGES - 2 and not last:
                            split(t + 1, range(MIDDLE))
                        gate_functions(t, b)
                        if b == RANGES - 2 and not last:
                            split(t + 1, range(MIDDLE, EARLY))

                with act.Fori(1, STEPS - 1) as t:
                    step(t, last=False)
                step(STEPS - 1, last=True)
            with act.Else():
                act.sem_inc(h_ready, RANGES)
                with act.Fori(0, STEPS) as t:
                    act.wait_ge(gs_summed, t + 1)
                    last = nc.scalar.activation(g_agg.rearrange("p (r c) -> p r c", r=RANGES), PS[:, :, 0:RB], ACT.Copy)
                    last.then_inc(gs_agg_kept, 1)
                    for b in range(RANGES):
                        act.wait_ge(gs_gates_made, t * RANGES + (b + 1))
                        nc.scalar.activation(gate_r, PS[:, 2, 0:RB], ACT.Sigmoid, bias=brz[:, 0:1])
                        nc.scalar.activation(gate_z, PS[:, 3, 0:RB], ACT.Sigmoid, bias=brz[:, 1:2]).then_inc(gs_rz_ready, 1)
                        act.wait_ge(gs_pre_ready, t * RANGES + (b + 1))
                        nc.scalar.activation(cand, pre_n, ACT.Tanh, bias=bih[:, 2:3]).then_inc(gs_cand_ready, 1)
            act.wait_ge(mv_made, KT)
            nc.scalar.activation(std[:, 0:KT - 1], mv[:, 0:KT - 1, 1], ACT.Sqrt, bias=eps)
            nc.scalar.activation(std[0:KLAST, KT - 1:KT], mv[0:KLAST, KT - 1:KT, 1], ACT.Sqrt,
                                 bias=eps[0:KLAST, :]).then_inc(std_made, 1)

        @block.vector
        def _(dve):
            order = [0]

            def link(ins):
                order[0] += 1
                ins.then_inc(prep_chain, 1)
                dve.wait_ge(prep_chain, order[0])

            dve.wait_ge(dst_in, 16)
            link(nc.vector.tensor_copy(first_dst, dst_rows[0:DR, 0:1]))

            def message(t, u):
                w, n = width(u)
                dve.wait_ge(msg_made, t * UNITS + (u + 1))
                dve.wait_ge(rest_done, t * UNITS + (u + 1))
                nc.vector.tensor_tensor(msg32[u % 2][0:n, 0:w, :],
                                        PS[0:n, MSG_BANKS[u % 2], 0:w * H].rearrange("p (k h) -> p k h", k=w),
                                        bmsg[0:n, :].unsqueeze(1).to_broadcast([n, w, H]),
                                        ALU.add).then_inc(msg32_ready, 1)

            def messages(t, units):
                for u in units:
                    w, n = width(u)
                    if u == units[0]:
                        message(t, u)
                    if u < units[-1]:
                        message(t, u + 1)
                    dve.wait_ge(part1_done, t * UNITS + (u + 1))
                    dve.wait_ge(parts_ready, t * UNITS + (u + 1))
                    nc.vector.tensor_tensor(rest[u % 2][0:n, 0:w, :], msg32[u % 2][0:n, 0:w, :],
                                            parts[0:n, 2 * u:2 * u + w, 0, :], ALU.subtract).then_inc(rest_done, 1)

            dve.sem_inc(msg32_ready, 2)
            dve.sem_inc(parts_ready, 2)
            dve.sem_inc(rest_done, 2)
            dve.wait_ge(consts_made, 1)
            nc.vector.tensor_scalar(below[0:DR, :], thr_row[0:DR, :], first_dst, None, ALU.is_gt).then_inc(below_made, 1)
            dve.wait_ge(rows_counted, 1)
            link(nc.vector.tensor_scalar(row_f, PS[0:GS, 0, 0:SETS], -1.0, 0.0, ALU.add, ALU.max))
            nc.vector.tensor_copy(row_i, row_f).then_inc(rows_set, 1)
            dve.wait_ge(b_in, 48)
            nc.vector.tensor_tensor(brz[:, :], bih[:, 0:2], bhh[:, 0:2], ALU.add)
            messages(0, range(SPLIT0))
            dve.wait_ge(rows_in, 32)
            for s in range(SETS):
                last = nc.vector.tensor_scalar(key[0:GS, :, :].rearrange("p s w -> p (s w)")[:, 0:DW], row_of[0:GS, s, :],
                                               thr_part[:, s:s + 1], 0.0, ALU.is_lt, ALU.add,
                                               accum_out=before[:, s:s + 1])
                link(last)
            link(nc.vector.scalar_tensor_tensor(out=start_f, in0=row_f, scalar=float(DW), in1=before,
                                                op0=ALU.mult, op1=ALU.add))
            nc.vector.tensor_scalar(start_i, start_f, float(E - WIN), None, ALU.min).then_inc(starts_set, 1)
            messages(0, range(SPLIT0, UNITS))
            for s in range(SETS):
                v2 = rng[0:GS, s, :]
                d, r, k, v, a, w = (t[0:GS, s, :] for t in (win_dst, win_src, key, valid, rng, rowin))
                r2, r3 = place_c[0:GS, :], place_q[0:GS, :]
                dve.wait_ge(windows_in[s], 32)
                link(nc.vector.tensor_scalar(k, d, thr_part[:, s:s + 1], None, ALU.subtract))
                link(nc.vector.tensor_scalar(v, k, 0.0, None, ALU.is_ge))
                link(nc.vector.scalar_tensor_tensor(out=v, in0=k, scalar=float(GROUP), in1=v, op0=ALU.is_lt,
                                                    op1=ALU.mult, accum_out=matched[:, s:s + 1]))
                link(nc.vector.tensor_scalar(r2, r, GROUP - 1, None, ALU.bitwise_and))
                link(nc.vector.tensor_scalar(r3, r, 4, GT - 1, ALU.logical_shift_right, ALU.bitwise_and))
                link(nc.vector.scalar_tensor_tensor(out=w, in0=r2, scalar=float(GT - 1), in1=r, op0=ALU.mult, op1=ALU.add))
                link(nc.vector.scalar_tensor_tensor(out=w, in0=r3, scalar=-float(GROUP - 1), in1=w, op0=ALU.mult,
                                                    op1=ALU.add))
                link(nc.vector.scalar_tensor_tensor(out=v2, in0=r, scalar=float((KT - 1) * P), in1=r2, op0=ALU.is_ge,
                                                    op1=ALU.mult))
                link(nc.vector.scalar_tensor_tensor(out=w, in0=v2, scalar=-float(GT - GLAST), in1=w, op0=ALU.mult,
                                                    op1=ALU.add))
                link(nc.vector.tensor_scalar(a, w, float(RB), None, ALU.is_ge))
                for m in range(2, RANGES):
                    link(nc.vector.scalar_tensor_tensor(out=a, in0=w, scalar=float(m * RB), in1=a,
                                                        op0=ALU.is_ge, op1=ALU.add))
                link(nc.vector.scalar_tensor_tensor(out=w, in0=a, scalar=-float(RB), in1=w, op0=ALU.mult, op1=ALU.add))
                link(nc.vector.scalar_tensor_tensor(out=k, in0=a, scalar=float(GROUP), in1=k, op0=ALU.mult, op1=ALU.add))
                last = nc.vector.scalar_tensor_tensor(out=k, in0=k, scalar=1.0, in1=v, op0=ALU.add, op1=ALU.mult)
                last.then_inc(keys_made, 1)
                dve.wait_ge(keys_made, s + 1)
            nc.vector.tensor_copy(matched, matched).then_inc(matched_made, 1)
            dve.wait_ge(parts_ready, UNITS + 2)
            for s in range(SETS):
                dve.wait_ge(keys_turned, s + 1)
                for a, t in enumerate((keyT, rowT)):
                    last = nc.vector.tensor_copy(
                        t[:, s * GS * CHUNKS:(s + 1) * GS * CHUNKS].rearrange("p (g c) -> p c g", c=CHUNKS),
                        PS[:, (0, 1, 4, 5)[2 * s + a], 0:CHUNKS * GS].rearrange("p (c g) -> p c g", c=CHUNKS))
            link(last)
            dve.wait_ge(matched_summed, 1)
            nc.vector.tensor_scalar(flag[0:1, 0:1], PS[0:1, 7, 0:1], float(E), None, ALU.is_equal).then_inc(flag_set, 1)
            dve.wait_ge(x_kept, -(-KT // 4))
            dve.wait_ge(consts_made, 3)
            dve.wait_ge(flag_set, 1)
            fast = dve.value_load(flag[0:1, 0:1], min_val=0, max_val=1)
            with dve.If(fast == 1):
                def one_hots(g, q):
                    dve.wait_ge(counted, g + (q + (2 if q % PAIR == 0 else 1)))
                    if q % PAIR == 0:
                        nc.vector.tensor_tensor(
                            hot_key[:, q // PAIR % 2, :, :], iota_key.rearrange("p (m c) -> p m c", m=P),
                            keyT[:, bass.ds((g + q) * CHUNKS, PAIR * CHUNKS)].unsqueeze(1).to_broadcast(
                                [P, P, PAIR * CHUNKS]), ALU.is_equal)
                    for c in range(CHUNKS):
                        last = nc.vector.tensor_scalar(hot_row[q % RING][:, c, :], iota_row,
                                                       rowT[:, bass.ds((g + q) * CHUNKS + c, 1)], None, ALU.is_equal)
                    last.then_inc(hots_ready, 1)

                dve.sem_inc(counted, RING)
                with dve.Fori(0, (KT - 1) // 2) as i:
                    for q in range(2 * GT):
                        one_hots(i * (2 * GT), q)
                for q in range(GLAST):
                    one_hots((KT - 1) * GT, q)
                dve.sem_inc(pre_ready, 1)

                def update(t, b):
                    c = t * RANGES
                    hb = hT[:, b * RB:(b + 1) * RB]
                    dve.wait_ge(n_made, c + (b + 1))
                    dve.wait_ge(rz_ready, c + (b + 2))
                    nc.vector.scalar_tensor_tensor(out=pre_n, in0=PS[:, HN_BANK, 0:RB], scalar=bhh[:, 2:3], in1=gate_r,
                                                   op0=ALU.add, op1=ALU.mult).then_inc(n_half, 1)
                    dve.wait_ge(n_half, c + (b + 1))
                    nc.vector.tensor_tensor(pre_n, PS[:, IN_BANK, 0:RB], pre_n, ALU.add).then_inc(pre_ready, 1)
                    dve.wait_ge(cand_ready, c + (b + 1))
                    nc.vector.tensor_tensor(diff, hb, cand, ALU.subtract).then_inc(d_made, 1)
                    dve.wait_ge(d_made, c + (b + 1))
                    nc.vector.tensor_tensor(diff, gate_z, diff, ALU.mult).then_inc(zd_made, 1)
                    dve.wait_ge(zd_made, c + (b + 1))
                    nc.vector.tensor_tensor(hb, cand, diff, ALU.add).then_inc(h_ready, 1)

                made = 0
                for b in range(RANGES):
                    update(0, b)
                    if b >= RANGES // 2:
                        ready = units_within(b)
                        messages(1, range(made, ready))
                        made = ready

                def step(t, last):
                    messages(t, range(LATE, UNITS))
                    for b in range(RANGES):
                        if b == RANGES - 1 and not last:
                            messages(t + 1, range(EARLY, LATE))
                        if b == RANGES - 2 and not last:
                            messages(t + 1, range(MIDDLE))
                        update(t, b)
                        if b == RANGES - 2 and not last:
                            messages(t + 1, range(MIDDLE, EARLY))

                with dve.Fori(1, STEPS - 1) as t:
                    step(t, last=False)
                step(STEPS - 1, last=True)
            with dve.Else():
                dve.wait_ge(gs_src_in, 16)
                nc.vector.tensor_scalar(g_c[0:DR, :], g_src[0:DR, :], GROUP - 1, None, ALU.bitwise_and)
                nc.vector.tensor_scalar(g_q[0:DR, :], g_src[0:DR, :], 4, GT - 1, ALU.logical_shift_right,
                                        ALU.bitwise_and).then_inc(gs_rows, 1)
                dve.wait_ge(gs_rows, 1)
                nc.vector.scalar_tensor_tensor(out=g_row[0:DR, :], in0=g_c[0:DR, :], scalar=float(GT - 1),
                                               in1=g_src[0:DR, :], op0=ALU.mult, op1=ALU.add).then_inc(gs_rows, 1)
                dve.wait_ge(gs_rows, 2)
                nc.vector.scalar_tensor_tensor(out=g_row[0:DR, :], in0=g_q[0:DR, :], scalar=-float(GROUP - 1),
                                               in1=g_row[0:DR, :], op0=ALU.mult, op1=ALU.add).then_inc(gs_rows, 1)
                nc.vector.scalar_tensor_tensor(out=g_last[0:DR, :], in0=g_src[0:DR, :], scalar=float((KT - 1) * P),
                                               in1=g_c[0:DR, :], op0=ALU.is_ge, op1=ALU.mult).then_inc(gs_rows, 1)
                dve.wait_ge(gs_rows, 4)
                nc.vector.scalar_tensor_tensor(out=g_row[0:DR, :], in0=g_last[0:DR, :], scalar=-float(GT - GLAST),
                                               in1=g_row[0:DR, :], op0=ALU.mult, op1=ALU.add).then_inc(gs_rows, 1)
                dve.wait_ge(gs_rows, 5)
                dve.wait_ge(gs_consts, 1)
                dve.sem_inc(gs_used, 1)
                dve.sem_inc(gs_msg_kept, 1)
                dve.sem_inc(gs_msg_stored, 16)
                with dve.Fori(0, STEPS) as t:
                    for u in range(MU):
                        w = min(4, KT - 4 * u)
                        dve.wait_ge(gs_msg_made, t * MU + (u + 1))
                        if u == 0:
                            dve.wait_ge(gs_msg_stored, t * (16 * MOVES) + 16)
                        n = KLAST if w == 1 else P
                        nc.vector.tensor_tensor(g_msg[0:n, 4 * u:4 * u + w, :],
                                                PS[0:n, 0, 0:w * H].rearrange("p (k h) -> p k h", k=w),
                                                bmsg[0:n, :].unsqueeze(1).to_broadcast([n, w, H]),
                                                ALU.add).then_inc(gs_msg_kept, 1)
                    with dve.Fori(0, DW) as e:
                        dve.wait_ge(gs_used, t * DW + (e + 1))
                        nc.vector.tensor_copy(g_index[0:DR, :], dst_rows[0:DR, bass.ds(e, 1)]).then_inc(gs_index, 1)
                        nc.vector.tensor_scalar(g_hot[0:DR, :], g_iota[0:DR, :], g_row[0:DR, bass.ds(e, 1)], None,
                                                ALU.is_equal).then_inc(gs_hot, 1)
                    for b in range(RANGES):
                        c = t * RANGES
                        hb = hT[:, b * RB:(b + 1) * RB]
                        dve.wait_ge(gs_rz_ready, c + (b + 1))
                        nc.vector.scalar_tensor_tensor(out=pre_n, in0=PS[:, 4, 0:RB], scalar=bhh[:, 2:3], in1=gate_r,
                                                       op0=ALU.add, op1=ALU.mult).then_inc(gs_half, 1)
                        dve.wait_ge(gs_half, c + (b + 1))
                        nc.vector.tensor_tensor(pre_n, PS[:, 5, 0:RB], pre_n, ALU.add).then_inc(gs_pre_ready, 1)
                        dve.wait_ge(gs_cand_ready, c + (b + 1))
                        nc.vector.tensor_tensor(diff, hb, cand, ALU.subtract).then_inc(gs_d_made, 1)
                        dve.wait_ge(gs_d_made, c + (b + 1))
                        nc.vector.tensor_tensor(diff, gate_z, diff, ALU.mult).then_inc(gs_zd_made, 1)
                        dve.wait_ge(gs_zd_made, c + (b + 1))
                        nc.vector.tensor_tensor(hb, cand, diff, ALU.add).then_inc(h_ready, 1)
            dve.wait_ge(x2_in, 16 * MOVES)
            for g in range(-(-KT // 4)):
                w = min(4, KT - 4 * g)
                n = KLAST if w == 1 else P
                dve.wait_ge(out_turned, g + 1)
                nc.vector.tensor_tensor(y[0:n, 4 * g:4 * g + w, :], y[0:n, 4 * g:4 * g + w, :],
                                        PS[0:n, 4 + g % 4, 0:w * P].rearrange("p (k h) -> p k h", k=w),
                                        ALU.add).then_inc(y_made, 1)
                dve.wait_ge(y_made, g + 1)
                for k in range(4 * g, 4 * g + w):
                    nc.vector.bn_stats(stats[0:n, k, :], y[0:n, k, :]).then_inc(stats_made, 1)
            for k in range(KT):
                n = KLAST if k == KT - 1 else P
                dve.wait_ge(stats_made, k + 1)
                nc.vector.bn_aggr(mv[0:n, k, :], stats[0:n, k, :]).then_inc(mv_made, 1)
            dve.wait_ge(std_made, 1)
            nc.vector.reciprocal(rstd[:, 0:KT - 1], std[:, 0:KT - 1])
            nc.vector.reciprocal(rstd[0:KLAST, KT - 1:KT], std[0:KLAST, KT - 1:KT]).then_inc(rstd_made, 1)
            dve.wait_ge(rstd_made, 1)
            for k in range(KT):
                n = KLAST if k == KT - 1 else P
                nc.vector.tensor_scalar(res[0:n, k, :], y[0:n, k, :], mv[0:n, k, 0:1], rstd[0:n, k:k + 1],
                                        ALU.subtract, ALU.mult).then_inc(res_made, 1)


_INS = ['x', 'src', 'dst', 'L0_gnn_W_msg', 'L0_gnn_b_msg', 'L0_gnn_W_ih', 'L0_gnn_W_hh', 'L0_gnn_b_ih', 'L0_gnn_b_hh']


def kernel(**inputs):
    import numpy as _np
    import concourse.bacc as _bacc
    from concourse import mybir as _mybir
    from concourse.bass_utils import run_bass_kernel_spmd as _run

    nc = _bacc.Bacc("TRN2", target_bir_lowering=False, num_devices=1, dynamic_dma_scratch_size=8192)
    arrays, args = {}, []
    for name in _INS:
        a = _np.ascontiguousarray(inputs[name])
        arrays[f"in_{name}"] = a
        args.append(nc.dram_tensor(f"in_{name}", a.shape, _mybir.dt.from_np(a.dtype), kind="ExternalInput").ap())
    args.append(nc.dram_tensor("out", inputs['x'].shape, _mybir.dt.float32, kind="ExternalOutput").ap())
    gnn_kernel(nc, *args)
    r = _run(nc, [arrays], core_ids=[0])
    return r.results[0]["out"]
```

```python
from contextlib import ExitStack

import concourse.bass as bass
from concourse import mybir

ALU = mybir.AluOpType
ACT = mybir.ActivationFunctionType
F32 = mybir.dt.float32
F16 = mybir.dt.float16
BF16 = mybir.dt.bfloat16
I32 = mybir.dt.int32

P = 128
H = 128
STEPS = 5
EPS = 1e-5
ROUND = 1.5 * 2.0 ** 23
GROUP = 16
RANGES = P // GROUP
WIN = 384
CHUNKS = WIN // P
BANKS = 8
BANK = 512
PAIR = 2
LAG = 2
COUNT_BANKS = (6, 7)
RING = 4
R_BANK, Z_BANK, IN_BANK, HN_BANK = 0, 1, 2, 7
AGG_BANKS = (4, 5)
MSG_BANKS = (3, 6)


def gnn_kernel(nc, x, src, dst, w_msg, b_msg, w_ih, w_hh, b_ih, b_hh, out):
    N = x.shape[0]
    E = src.shape[0]
    KT = -(-N // P)
    GT = P // GROUP
    TAIL = N - (KT - 1) * P
    GLAST = -(-TAIL // GROUP)
    KLAST = GLAST * GROUP
    NG = (KT - 1) * GT + GLAST
    SETS = 2
    GS = NG // SETS
    RB = NG * GROUP // RANGES
    NP = RANGES * RB
    DR = 125
    DW = E // DR
    UNITS = -(-KT // 2)
    BLOCKS = NP // BANK
    REST = NP - BLOCKS * BANK
    assert GS * SETS == NG and NP == NG * GROUP and NP >= N and DR * DW == E and REST > 0
    assert (KT - 1) % 2 == 0 and BLOCKS == COUNT_BANKS[0] and 2 * KLAST == P

    with ExitStack() as ctx:
        def sb(name, shape, dt):
            return ctx.enter_context(nc.sbuf_tensor(name, shape, dt))

        def sem(name):
            return ctx.enter_context(nc.semaphore(name))

        A = sb("A", [P, KT, NP], F16)
        parts = sb("parts", [P, KT, 3, H], BF16)
        hT = sb("hT", [P, NP], F32)
        scratch = sb("scratch", [P, 6656], F32)
        ident = sb("ident", [P, P], F32)
        wT = sb("wT", [P, 7, P], F32)
        bmsg = sb("bmsg", [P, H], F32)
        bih = sb("bih", [P, 3], F32)
        bhh = sb("bhh", [P, 3], F32)
        brz = sb("brz", [P, 2], F32)
        ones = sb("ones", [P, 1], F32)
        small = sb("small", [P, 16], F32)
        smalli = sb("smalli", [P, 8], I32)
        flag = sb("flag", [1, 1], I32)

        PS = ctx.enter_context(nc.psum_tensor("PS", [P, BANKS, BANK], F32))

        def view(t, lo, n, dt=F32):
            size = 2 if dt in (F16, BF16) else 4
            own = 2 if t.dtype in (F16, BF16) else 4
            flat = t[:, lo // own:(lo + n * size) // own]
            return flat if dt == t.dtype else flat.bitcast(dt)

        class Flat:
            def __init__(self, ap, dt):
                self.ap, self.dtype = ap, dt

            def __getitem__(self, k):
                return self.ap[k]

        A_flat = Flat(A[:, :, :].rearrange("p k n -> p (k n)"), F16)
        parts_flat = Flat(parts[:, :, :, :].rearrange("p k t h -> p (k t h)"), BF16)
        s_flat = Flat(scratch[:, :], F32)

        at = [(KT - 5) * NP * 2]

        def prep(n, dt):
            v = view(A_flat, at[0], n, dt)
            at[0] += n * 4
            return v

        dst_rows = prep(DW, I32)
        below = prep(NG, F32)
        thr_row = prep(NG, F32)
        row_of = prep(SETS * DW, I32).rearrange("p (s w) -> p s w", s=SETS)
        win_dst = prep(SETS * WIN, I32).rearrange("p (s w) -> p s w", s=SETS)
        win_src = prep(SETS * WIN, I32).rearrange("p (s w) -> p s w", s=SETS)
        key = prep(SETS * WIN, F32).rearrange("p (s w) -> p s w", s=SETS)
        valid = prep(SETS * WIN, F32).rearrange("p (s w) -> p s w", s=SETS)
        rng = prep(SETS * WIN, F32).rearrange("p (s w) -> p s w", s=SETS)
        rowin = prep(SETS * WIN, F32).rearrange("p (s w) -> p s w", s=SETS)
        place_c, place_q = prep(WIN, I32), prep(WIN, I32)
        assert at[0] <= KT * NP * 2
        x_nodes = view(A_flat, 0, KT * H, F32).rearrange("p (k h) -> p k h", k=KT)
        w_raw = view(A_flat, KT * H * 4, 7 * P, F32).rearrange("p (g h) -> p g h", g=7)
        at1 = [0]

        def counting(n, dt):
            v = view(s_flat, at1[0], n, dt)
            at1[0] += n * (2 if dt == F16 else 4)
            return v

        stage = counting(2 * GT * RB, F16).rearrange("p (s q r) -> p s q r", s=2, q=GT)
        rowT = counting(NG * CHUNKS, F32)
        keyT = counting(NG * CHUNKS, F16)
        iota_row = counting(RB, F16)
        iota_key = counting(P * PAIR * CHUNKS, F16)
        hot_key = counting(2 * P * PAIR * CHUNKS, F16).rearrange("p (s m c) -> p s m c", s=2, m=P)
        hot_row = [v.rearrange("p (c w) -> p c w", c=CHUNKS) for v in (
            counting(CHUNKS * RB, F16), counting(CHUNKS * RB, F16),
            view(A_flat, (KT - 1) * NP * 2, CHUNKS * RB, F16),
            view(A_flat, (KT - 1) * NP * 2 + CHUNKS * RB * 2, CHUNKS * RB, F16))]
        assert at1[0] <= 6656 * 4
        at2 = [0]

        def work(n):
            v = view(s_flat, at2[0], n, F32)
            at2[0] += 4 * n
            return v

        agg = work(NP)
        gate_r, pre_n, cand, diff = (work(RB) for _ in range(4))
        gate_z = [work(RB) for _ in range(2)]
        msg32 = [work(2 * H).rearrange("p (k h) -> p k h", k=2) for _ in range(2)]
        rest = [work(2 * H).rearrange("p (k h) -> p k h", k=2) for _ in range(2)]
        assert at2[0] <= 6656 * 4
        A_tiles = A[:, :, :].rearrange("p k n -> p (k n)").bitcast(F32).rearrange("p (k n) -> p k n", k=KT)
        y = A_tiles[:, :, 0:H]
        res = A_tiles[:, :, RB // 2:RB // 2 + H]
        stats = A_tiles[:, :, RB:RB + 6]
        mv = A_tiles[:, :, RB + 8:RB + 10]
        std = A_tiles[:, :, RB + 10:RB + 11]
        rstd = A_tiles[:, :, RB + 12:RB + 13]
        assert H * 2 <= RB
        at3 = [0]

        def gen(n, dt=F32):
            v = view(A_flat, at3[0], n, dt)
            at3[0] += 4 * n
            return v

        g_msg = gen(KT * H).rearrange("p (k h) -> p k h", k=KT)
        g_agg, g_iota, g_hot = gen(NP), gen(NP), gen(NP)
        g_src, g_c, g_q = gen(DW, I32), gen(DW, I32), gen(DW, I32)
        g_row, g_last, g_edge, g_zero = gen(DW), gen(DW), gen(H), gen(P)
        g_index, g_idle = gen(1, I32), gen(2)
        assert at3[0] <= (KT - 5) * NP * 2

        thr_part = small[0:GS, 0:2]
        row_f = small[0:GS, 2:4]
        before = small[0:GS, 4:6]
        matched = small[0:GS, 6:8]
        start_f = small[0:GS, 8:10]
        first_dst = small[0:DR, 10:11]
        eps = small[:, 11:12]
        row_i = smalli[0:GS, 0:2]
        start_i = smalli[0:GS, 2:4]

        dst_in, x_in, w_in, b_in = (sem(n) for n in ("dst_in", "x_in", "w_in", "b_in"))
        tail_zeroed, zeroed, consts_made = sem("tail_zeroed"), sem("zeroed"), sem("consts_made")
        prep_chain = sem("prep_chain")
        below_made, rows_counted, rows_set, rows_in = (sem(n) for n in ("below_made", "rows_counted", "rows_set", "rows_in"))
        starts_set, windows_in = sem("starts_set"), [sem("windows_in0"), sem("windows_in1")]
        keys_made, keys_turned, slots_kept, matched_made, matched_summed, flag_set = (
            sem(n) for n in ("keys_made", "keys_turned", "slots_kept", "matched_made", "matched_summed", "flag_set"))
        w_turned, w_kept, x_turned, x_kept = (sem(n) for n in ("w_turned", "w_kept", "x_turned", "x_kept"))
        hots_ready, counted, count_kept = sem("hots_ready"), sem("counted"), sem("count_kept")
        stored = [sem("stored0"), sem("stored1")]
        doubled = sem("doubled")
        h_ready, msg_made, msg32_ready, part1_done, rest_done, part2_done, parts_ready = (
            sem(n) for n in ("h_ready", "msg_made", "msg32_ready", "part1_done", "rest_done", "part2_done", "parts_ready"))
        first_made, agg_made, agg_kept, rz_made, n_made, rz_ready, n_half, pre_ready, cand_ready, d_made, zd_made = (
            sem(n) for n in ("first_made", "agg_made", "agg_kept", "rz_made", "n_made", "rz_ready", "n_half", "pre_ready",
                             "cand_ready", "d_made", "zd_made"))
        y_zeroed, x2_in, out_turned, y_made, stats_made, mv_made, std_made, rstd_made, res_made, out_stored, tail_stored = (
            sem(n) for n in ("y_zeroed", "x2_in", "out_turned", "y_made", "stats_made", "mv_made", "std_made",
                             "rstd_made", "res_made", "out_stored", "tail_stored"))

        gs_src_in, gs_idle, gs_consts, gs_rows, gs_msg_made, gs_msg_kept, gs_msg_stored = (
            sem(n) for n in ("gs_src_in", "gs_idle", "gs_consts", "gs_rows", "gs_msg_made", "gs_msg_kept", "gs_msg_stored"))
        gs_index, gs_edges_in, gs_hot, gs_used, gs_summed, gs_agg_kept = (
            sem(n) for n in ("gs_index", "gs_edges_in", "gs_hot", "gs_used", "gs_summed", "gs_agg_kept"))
        gs_gates_made, gs_rz_ready, gs_half, gs_pre_ready, gs_cand_ready, gs_d_made, gs_zd_made = (
            sem(n) for n in ("gs_gates_made", "gs_rz_ready", "gs_half", "gs_pre_ready", "gs_cand_ready", "gs_d_made",
                             "gs_zd_made"))
        messages = nc.dram_tensor("messages", (N, H), F32, kind="Internal").ap()
        MU = -(-KT // 4)

        def by_place(nodes, tiles):
            whole = nodes[0:(KT - 1) * P, :].rearrange("(k q c) h -> q c k h", q=GT, c=GROUP)
            pairs = [(whole[q], tiles[q:P:GT, 0:KT - 1, :]) for q in range(GT)]
            for q in range(-(-TAIL // GROUP)):
                n = min(GROUP, TAIL - q * GROUP)
                first = (KT - 1) * P + q * GROUP
                pairs.append((nodes[first:first + n, :], tiles[q:q + GLAST * (n - 1) + 1:GLAST, KT - 1, :]))
            return pairs

        dst_2d = dst.rearrange("(a b) -> a b", b=DW)
        src_2d = src.rearrange("(a b) -> a b", b=DW)

        MOVES = GT + -(-TAIL // GROUP)

        def width(u):
            return min(2, KT - 2 * u)

        def slots(k):
            return ((0, P), (2, KLAST)) if k == KT - 1 else ((0, P), (1, P), (2, P))

        def first_units(b):
            return range(units_within(b - 2), units_within(b - 1)) if b >= 2 else range(0)

        def units_within(ranges):
            return min(UNITS - 1, ranges * RB // (2 * P))

        QUADS = -(-KT // 4)
        EARLY_QUADS = 4

        def quad(g):
            return range(4 * g, min(4 * g + 4, KT)), (KLAST if 4 * g == KT - 1 else P)

        def quad_ranges(g):
            return -(-min(4 * (g + 1) * P, NP) // RB)

        EARLY = units_within(RANGES - 2)
        MIDDLE = EARLY // 2
        LATE = units_within(RANGES - 1)

        block = ctx.enter_context(nc.Block())

        @block.sync
        def _(sp):
            sp.dma_start(dst_rows[0:DR, :], dst_2d).then_inc(dst_in, 16)
            sp.wait_ge(tail_zeroed, 1)
            for nodes, places in by_place(x, x_nodes):
                sp.dma_start(places, nodes).then_inc(x_in, 16)
            sp.wait_ge(flag_set, 1)
            fast = sp.value_load(flag[0:1, 0:1], min_val=0, max_val=1)
            with sp.If(fast == 1):
                with sp.Fori(0, (KT - 1) // 2) as i:
                    for s in range(2):
                        sp.wait_ge(count_kept, i * (2 * GT) + (GT * (s + 1) + 2))
                        for r in range(RANGES):
                            sp.dma_start(
                                A[:, bass.ds(i * 2 + s, 1), r * RB:(r + 1) * RB].rearrange("p k n -> p (k n)"),
                                stage[r * GROUP:(r + 1) * GROUP, s, :, :]).then_inc(stored[s], 16)
                sp.wait_ge(count_kept, NG + 2)
                for r in range(RANGES):
                    sp.dma_start(A[0:KLAST, KT - 1, r * RB:(r + 1) * RB],
                                 stage[r * GROUP:(r + 1) * GROUP, 0, 0:GLAST, :]).then_inc(stored[0], 16)
                sp.wait_ge(stored[0], 16 * RANGES * ((KT - 1) // 2 + 2))
                sp.dma_start(A[KLAST:P, KT - 1, :], A[0:KLAST, KT - 1, :]).then_inc(doubled, 16)
                sp.wait_ge(agg_made, (STEPS - 2) * RANGES + 1)
                sp.wait_ge(y_zeroed, 1)
                for nodes, places in by_place(x, y):
                    sp.dma_start(places, nodes).then_inc(x2_in, 16)
            with sp.Else():
                sp.dma_start(g_src[0:DR, :], src_2d).then_inc(gs_src_in, 16)
                with sp.Fori(0, STEPS) as t:
                    sp.wait_ge(gs_msg_kept, t * MU + (MU + 1))
                    for nodes, places in by_place(messages, g_msg):
                        sp.dma_start(nodes, places).then_inc(gs_msg_stored, 16)
                sp.wait_ge(gs_msg_stored, 16 * MOVES * STEPS + 16)
                sp.wait_ge(gs_gates_made, STEPS * RANGES)
                sp.wait_ge(y_zeroed, 1)
                for nodes, places in by_place(x, y):
                    sp.dma_start(places, nodes).then_inc(x2_in, 16)
            early = 4 * EARLY_QUADS
            sp.wait_ge(res_made, early)
            whole = out[0:early * P, :].rearrange("(k q c) h -> q c k h", q=GT, c=GROUP)
            for q in range(GT):
                sp.dma_start(whole[q], res[q:P:GT, 0:early, :]).then_inc(out_stored, 16)
            for k in range(early, KT - 1):
                sp.wait_ge(res_made, k + 1)
                sp.dma_start(out[k * P:(k + 1) * P, :].rearrange("(q c) h -> c q h", q=GT, c=GROUP),
                             res[:, k, :]).then_inc(out_stored, 16)
            sp.wait_ge(out_stored, 16 * (GT + KT - 1 - early))

        @block.gpsimd
        def _(pool):
            nc.gpsimd.memset(x_nodes[:, KT - 1, :], 0.0).then_inc(tail_zeroed, 1)
            nc.gpsimd.iota(thr_row[0:DR, :], pattern=[[GROUP, NG]], base=0, channel_multiplier=0,
                           allow_small_or_imprecise_dtypes=True)
            nc.gpsimd.iota(thr_part, pattern=[[GROUP * GS, SETS]], base=0, channel_multiplier=GROUP,
                           allow_small_or_imprecise_dtypes=True)
            nc.gpsimd.memset(ones[:, :], 1.0).then_inc(consts_made, 1)
            nc.gpsimd.memset(ident[:, :], 0.0).then_inc(zeroed, 1)
            pool.wait_ge(zeroed, 1)
            nc.gpsimd.affine_select(out=ident[:, :], in_=ident[:, :], compare_op=ALU.not_equal, fill=1.0,
                                    base=0, pattern=[[-1, P]], channel_multiplier=1).then_inc(consts_made, 1)
            nc.gpsimd.iota(iota_row, pattern=[[1, RB]], base=0, channel_multiplier=0,
                           allow_small_or_imprecise_dtypes=True)
            nc.gpsimd.iota(iota_key, pattern=[[1, P], [0, PAIR * CHUNKS]], base=1, channel_multiplier=0,
                           allow_small_or_imprecise_dtypes=True)
            nc.gpsimd.memset(eps, EPS).then_inc(consts_made, 1)
            pool.wait_ge(rows_set, 1)
            for s in range(SETS):
                nc.gpsimd.indirect_dma_start(
                    out=row_of[0:GS, s, :], out_offset=None, in_=dst_2d,
                    in_offset=bass.IndirectOffsetOnAxis(ap=row_i[:, s:s + 1], axis=0)).then_inc(rows_in, 16)
            def third_part(t, u):
                w = width(u)
                n = P if w == 2 else KLAST
                pool.wait_ge(part2_done, t * UNITS + (u + 1))
                nc.gpsimd.tensor_tensor(parts[0:n, 2 * u:2 * u + w, 2, :], rest[u % 2][0:n, 0:w, :],
                                        parts[0:n, 2 * u:2 * u + w, 1, :], ALU.subtract).then_inc(parts_ready, 1)

            pool.wait_ge(starts_set, 1)
            for s in range(SETS):
                for data, to in ((dst_2d, win_dst), (src_2d, win_src)):
                    nc.gpsimd.indirect_dma_start(
                        out=to[0:GS, s, :], out_offset=None, in_=data,
                        in_offset=bass.IndirectOffsetOnAxis(ap=start_i[:, s:s + 1], axis=1)).then_inc(windows_in[s], 16)
            for u in range(UNITS):
                third_part(0, u)
            pool.wait_ge(flag_set, 1)
            fast = pool.value_load(flag[0:1, 0:1], min_val=0, max_val=1)
            with pool.If(fast == 1):
                with pool.Fori(1, STEPS) as t:
                    for u in range(UNITS):
                        third_part(t, u)
                pool.wait_ge(agg_made, (STEPS - 2) * RANGES + 1)
                nc.gpsimd.memset(y[:, KT - 1, :], 0.0).then_inc(y_zeroed, 1)
            with pool.Else():
                nc.gpsimd.iota(g_iota, pattern=[[1, NP]], base=0, channel_multiplier=0,
                               allow_small_or_imprecise_dtypes=True)
                nc.gpsimd.memset(g_zero, 0.0).then_inc(gs_consts, 1)

                def hold_wait(n):
                    pool.wait_ge(gs_idle, n)
                    nc.gpsimd.tensor_tensor(g_idle[:, 1:2], g_idle[:, 0:1], g_idle[:, 0:1], ALU.add).then_inc(gs_idle, 1)

                nc.gpsimd.memset(g_idle[:, 0:1], 0.0).then_inc(gs_idle, 1)
                with pool.Fori(0, STEPS) as t:
                    pool.wait_ge(gs_msg_stored, t * (16 * MOVES) + (16 * MOVES + 16))
                    hold_wait(t * (DW + 1) + 1)
                    with pool.Fori(0, DW) as e:
                        pool.wait_ge(gs_index, t * DW + (e + 1))
                        hold_wait(t * (DW + 1) + (e + 2))
                        nc.gpsimd.indirect_dma_start(
                            out=g_edge[0:DR, :], out_offset=None, in_=messages,
                            in_offset=bass.IndirectOffsetOnAxis(ap=g_index[0:DR, :], axis=0)).then_inc(gs_edges_in, 16)
                pool.wait_ge(gs_edges_in, 16 * DW * STEPS)
                pool.wait_ge(gs_gates_made, STEPS * RANGES)
                nc.gpsimd.memset(y[:, KT - 1, :], 0.0).then_inc(y_zeroed, 1)
            pool.wait_ge(res_made, KT)
            for nodes, places in by_place(out, res)[GT:]:
                pool.dma_start(nodes, places).then_inc(tail_stored, 16)
            pool.wait_ge(tail_stored, 16 * (MOVES - GT))

        @block.tensor
        def _(pe):
            def message(t, u):
                pe.wait_ge(msg32_ready, t * UNITS + (u + 1))
                for k in range(2 * u, 2 * u + width(u)):
                    for half in range(2 if k == KT - 1 else 1):
                        n = KLAST if k == KT - 1 else P
                        mm = pe.matmul(PS[half * n:(half + 1) * n, MSG_BANKS[u % 2], k % 2 * H:(k % 2 + 1) * H],
                                       hT[:, k * P:k * P + n], wT[:, 6, :], start=True, stop=True)
                mm.then_inc(msg_made, 1)

            def turn_back(g):
                tiles, n = quad(g)
                pe.wait_ge(h_ready, STEPS * RANGES + quad_ranges(g))
                if g >= 2:
                    pe.wait_ge(y_made, g - 1)
                for k in tiles:
                    mm = pe.transpose(PS[0:n, MSG_BANKS[g % 2], (k % 4) * P:(k % 4 + 1) * P],
                                      hT[:, k * P:k * P + n], ident[:, :])
                mm.then_inc(out_turned, 1)

            pe.wait_ge(consts_made, 1)
            pe.wait_ge(below_made, 1)
            for s in range(SETS):
                mm = pe.matmul(PS[0:GS, 0, s:s + 1], below[0:DR, s * GS:(s + 1) * GS], ones[0:DR, :],
                               start=True, stop=True)
            mm.then_inc(rows_counted, 1)
            pe.wait_ge(consts_made, 3)
            pe.wait_ge(w_in, 48)
            for g in range(7):
                mm = pe.transpose(PS[:, 6 + g // 4, (g % 4) * P:(g % 4 + 1) * P], w_raw[:, g, :], ident[:, :])
            mm.then_inc(w_turned, 1)
            pe.wait_ge(x_in, 16 * MOVES)
            for k in range(KT):
                b = k // 4
                if k % 4 == 0 and b >= 2:
                    pe.wait_ge(x_kept, b - 1)
                n = KLAST if k == KT - 1 else P
                mm = pe.transpose(PS[:, 4 + b % 2, (k % 4) * P:(k % 4) * P + n], x_nodes[0:n, k, :], ident[0:n, 0:n])
                if k % 4 == 3 or k == KT - 1:
                    mm.then_inc(x_turned, 1)
            pe.wait_ge(w_kept, 1)
            pe.wait_ge(x_kept, -(-KT // 4))
            for u in range(len(MSG_BANKS)):
                message(0, u)
            for s in range(SETS):
                pe.wait_ge(keys_made, s + 1)
                for a, t in enumerate((key, rowin)):
                    for c in range(CHUNKS):
                        mm = pe.transpose(PS[:, (0, 1, 4, 5)[2 * s + a], c * GS:(c + 1) * GS],
                                          t[0:GS, s, c * P:(c + 1) * P], ident[0:GS, 0:GS])
                mm.then_inc(keys_turned, 1)
            pe.wait_ge(matched_made, 1)
            for s in range(SETS):
                mm = pe.matmul(PS[0:1, 7, 0:1], matched[:, s:s + 1], ones[0:GS, :], start=(s == 0), stop=(s == 1))
            mm.then_inc(matched_summed, 1)
            for u in range(len(MSG_BANKS), UNITS):
                message(0, u)
            pe.wait_ge(flag_set, 1)
            fast = pe.value_load(flag[0:1, 0:1], min_val=0, max_val=1)
            with pe.If(fast == 1):
                def count(g, q):
                    pe.wait_ge(hots_ready, g + (q + 1))
                    pe.wait_ge(count_kept, g + (q + 1))
                    for c in range(CHUNKS):
                        mm = pe.matmul(PS[:, COUNT_BANKS[q % 2], 0:RB], hot_key[:, q // PAIR % 2, :, q % PAIR * CHUNKS + c],
                                       hot_row[q % RING][:, c, :], start=(c == 0), stop=(c == CHUNKS - 1))
                    mm.then_inc(counted, 1)

                def first_product(k, blocks, start=False, stop=False, n=P):
                    for j in blocks:
                        lo, hi = j * BANK, min((j + 1) * BANK, NP)
                        for part in range(3):
                            mm = pe.matmul(PS[:, j, 0:hi - lo],
                                           parts[0:n, bass.ds(k, 1), part, :].rearrange("p k h -> p (k h)"),
                                           A[0:n, bass.ds(k, 1), lo:hi].rearrange("p k h -> p (k h)"),
                                           start=start and part == 0, stop=stop and part == 2, skip_group_check=True)
                    return mm

                def counts_and_product(i, product=True, start=False):
                    for s in range(2):
                        for q in range(GT):
                            count(i * (2 * GT), s * GT + q)
                            if product:
                                if q == 0:
                                    pe.wait_ge(stored[s], i * (16 * RANGES) + 16 * RANGES)
                                if q < BLOCKS:
                                    first_product(i * 2 + (s - LAG), (q,), start=start and s == 0)

                pe.wait_ge(parts_ready, UNITS + 2)
                counts_and_product(0, product=False)
                counts_and_product(1, start=True)
                with pe.Fori(2, (KT - 1) // 2) as i:
                    counts_and_product(i)
                for q in range(GLAST):
                    count((KT - 1) * GT, q)
                    if q == 0:
                        pe.wait_ge(stored[0], 16 * RANGES * ((KT - 1) // 2 + 1))
                    if 2 * q < BLOCKS:
                        first_product(KT - 1 - LAG, range(2 * q, 2 * q + 2))
                pe.wait_ge(stored[1], 16 * RANGES * ((KT - 1) // 2 + 1))
                first_product(KT - 2, range(BLOCKS))
                pe.wait_ge(count_kept, NG + 2)
                for k in range(KT - 1):
                    first_product(k, (BLOCKS,), start=k == 0)
                pe.wait_ge(stored[0], 16 * RANGES * ((KT - 1) // 2 + 2))
                for j in range(BLOCKS + 1):
                    first_product(KT - 1, (j,), stop=True, n=KLAST).then_inc(first_made, 1)

                def messages(t, units, ranges):
                    pe.wait_ge(h_ready, t * RANGES + ranges)
                    for u in units:
                        message(t, u)

                def gates(t, b, units=()):
                    hb = hT[:, b * RB:(b + 1) * RB]
                    gb = agg[:, b * RB:(b + 1) * RB]
                    pe.wait_ge(agg_kept, t * RANGES + (b + 1))
                    pe.wait_ge(rz_ready, t * RANGES + (b + 1))
                    for g, bank in enumerate((R_BANK, Z_BANK)):
                        pe.matmul(PS[:, bank, 0:RB], wT[:, 3 + g, :], hb, start=True, stop=False)
                        mm = pe.matmul(PS[:, bank, 0:RB], wT[:, g, :], gb, start=False, stop=True)
                    mm.then_inc(rz_made, 1)
                    if len(units):
                        messages(t + 1, units, b - 1)
                    pe.wait_ge(pre_ready, t * RANGES + (b + 1))
                    pe.matmul(PS[:, HN_BANK, 0:RB], wT[:, 5, :], hb, start=True, stop=True)
                    pe.matmul(PS[:, IN_BANK, 0:RB], wT[:, 2, :], gb, start=True, stop=True).then_inc(n_made, 1)

                pe.wait_ge(agg_kept, IN_BANK + 1)
                for b in range(RANGES):
                    if b == 2:
                        pe.wait_ge(agg_kept, RANGES)
                    gates(0, b, first_units(b))

                def product(t, b, k):
                    for part, n in slots(k):
                        mm = pe.matmul(PS[:, AGG_BANKS[b % 2], 0:RB], parts[0:n, k, part, :],
                                       A[0:n, k, b * RB:(b + 1) * RB],
                                       start=(k == 0 and part == 0), stop=(k == KT - 1 and part == 2))
                    if k == KT - 1:
                        mm.then_inc(agg_made, 1)

                def step(t, last):
                    for b in range(RANGES):
                        for k in range(KT):
                            if last and k == KT // 2:
                                for g in range(QUADS):
                                    if quad_ranges(g) == b - 1:
                                        turn_back(g)
                            if b == 0 and k == 2:
                                messages(t, range(EARLY, LATE), RANGES - 1)
                            if b == 0 and k == KT // 2:
                                messages(t, range(LATE, UNITS), RANGES)
                            if b == 0 and k % 2 == 0:
                                pe.wait_ge(parts_ready, t * UNITS + (k // 2 + 1 + 2))
                            if b > 0 and k == KT // 2:
                                gates(t, b - 1)
                            product(t, b, k)
                            if b == RANGES - 1 and not last and k % 2 == 1 and 3 <= k < 2 * EARLY + 3:
                                messages(t + 1, (k // 2 - 1,), RANGES - 2)
                    if last:
                        turn_back(QUADS - 3)
                    gates(t, RANGES - 1)
                    if last:
                        turn_back(QUADS - 2)
                        turn_back(QUADS - 1)

                pe.wait_ge(doubled, 16)
                with pe.Fori(1, STEPS - 1) as t:
                    step(t, last=False)
                step(STEPS - 1, last=True)
            with pe.Else():
                pe.wait_ge(gs_consts, 1)
                pe.wait_ge(h_ready, RANGES)
                with pe.Fori(0, STEPS) as t:
                    pe.wait_ge(h_ready, t * RANGES + RANGES)
                    for u in range(MU):
                        pe.wait_ge(gs_msg_kept, t * MU + (u + 1))
                        for k in range(4 * u, min(4 * u + 4, KT)):
                            n = KLAST if k == KT - 1 else P
                            mm = pe.matmul(PS[0:n, 0, (k % 4) * H:(k % 4 + 1) * H], hT[:, k * P:k * P + n], wT[:, 6, :],
                                           start=True, stop=True)
                        mm.then_inc(gs_msg_made, 1)
                    pe.wait_ge(gs_msg_kept, t * MU + (MU + 1))
                    for r in range(RANGES):
                        pe.matmul(PS[:, r, 0:RB], g_zero, g_iota[:, 0:RB], start=True, stop=False, skip_group_check=True)
                    with pe.Fori(0, DW) as e:
                        pe.wait_ge(gs_edges_in, t * (16 * DW) + e * 16 + 16)
                        pe.wait_ge(gs_hot, t * DW + (e + 1))
                        for r in range(RANGES):
                            mm = pe.matmul(PS[:, r, 0:RB], g_edge[0:DR, :], g_hot[0:DR, r * RB:(r + 1) * RB],
                                           start=False, stop=False, skip_group_check=True)
                        mm.then_inc(gs_used, 1)
                    for r in range(RANGES):
                        mm = pe.matmul(PS[:, r, 0:RB], g_zero, g_iota[:, 0:RB], start=False, stop=True,
                                       skip_group_check=True)
                    mm.then_inc(gs_summed, 1)
                    pe.wait_ge(gs_agg_kept, t + 1)
                    for b in range(RANGES):
                        hb, gb = hT[:, b * RB:(b + 1) * RB], g_agg[:, b * RB:(b + 1) * RB]
                        pe.wait_ge(h_ready, t * RANGES + (RANGES + b))
                        for g in range(2):
                            pe.matmul(PS[:, 2 + g, 0:RB], wT[:, 3 + g, :], hb, start=True, stop=False)
                            pe.matmul(PS[:, 2 + g, 0:RB], wT[:, g, :], gb, start=False, stop=True)
                        pe.matmul(PS[:, 4, 0:RB], wT[:, 5, :], hb, start=True, stop=True)
                        pe.matmul(PS[:, 5, 0:RB], wT[:, 2, :], gb, start=True, stop=True).then_inc(gs_gates_made, 1)
                pe.wait_ge(h_ready, STEPS * RANGES + RANGES)
                for g in range(QUADS):
                    turn_back(g)

        @block.scalar
        def _(act):
            act.dma_start(w_raw[:, 0:3, :], w_ih.rearrange("(g p) h -> p g h", p=P)).then_inc(w_in, 16)
            act.dma_start(w_raw[:, 3:6, :], w_hh.rearrange("(g p) h -> p g h", p=P)).then_inc(w_in, 16)
            act.dma_start(w_raw[:, 6, :], w_msg).then_inc(w_in, 16)
            act.dma_start(bmsg[:, :], bass.AP(tensor=b_msg.tensor, offset=b_msg.offset,
                                              ap=[[0, P], [1, H]])).then_inc(b_in, 16)
            with nc.allow_non_contiguous_dma(reason="biases to partitions, 384 numbers each"):
                act.dma_start(bih[:, :], b_ih.rearrange("(g p) -> p g", p=P)).then_inc(b_in, 16)
                act.dma_start(bhh[:, :], b_hh.rearrange("(g p) -> p g", p=P)).then_inc(b_in, 16)
            act.wait_ge(w_turned, 1)
            nc.scalar.activation(wT[:, 0:4, :], PS[:, 6, :].rearrange("p (g h) -> p g h", g=4), ACT.Copy)
            nc.scalar.activation(wT[:, 4:7, :], PS[:, 7, 0:3 * P].rearrange("p (g h) -> p g h", g=3),
                                 ACT.Copy).then_inc(w_kept, 1)
            for b in range(-(-KT // 4)):
                n = min(4 * P, NP - 4 * b * P)
                act.wait_ge(x_turned, b + 1)
                nc.scalar.activation(hT[:, 4 * b * P:4 * b * P + n], PS[:, 4 + b % 2, 0:n],
                                     ACT.Copy).then_inc(x_kept, 1)

            def part(t, u, j):
                w = width(u)
                n = P if w == 2 else KLAST
                if j == 0:
                    act.wait_ge(msg32_ready, t * UNITS + (u + 1 + 2))
                    nc.scalar.activation(parts[:, 2 * u:2 * u + w, 0, :], msg32[u % 2][:, 0:w, :],
                                         ACT.Copy).then_inc(part1_done, 1)
                else:
                    act.wait_ge(rest_done, t * UNITS + (u + 1 + 2))
                    if n < P:
                        nc.scalar.activation(parts[n:P, 2 * u:2 * u + w, 0, :], rest[u % 2][n:P, 0:w, :], ACT.Copy)
                    nc.scalar.activation(parts[0:n, 2 * u:2 * u + w, 1, :], rest[u % 2][0:n, 0:w, :],
                                         ACT.Copy).then_inc(part2_done, 1)

            def split(t, units):
                for u in units:
                    if u == units[0]:
                        part(t, u, 0)
                    if u < units[-1]:
                        part(t, u + 1, 0)
                    part(t, u, 1)

            def deviation(first, past):
                for g in range(first, past):
                    tiles, n = quad(g)
                    a, z = tiles[0], tiles[-1] + 1
                    act.wait_ge(mv_made, z)
                    last = nc.scalar.activation(std[0:n, a:z, 0], mv[0:n, a:z, 1], ACT.Sqrt, bias=eps[0:n, :])
                    last.then_inc(std_made, 1)

            def keep_slots(s):
                act.wait_ge(keys_turned, s + 1)
                for a, t in enumerate((keyT, rowT)):
                    nc.scalar.activation(
                        t[:, s * GS * CHUNKS:(s + 1) * GS * CHUNKS].rearrange("p (g c) -> p c g", c=CHUNKS),
                        PS[:, (0, 1, 4, 5)[2 * s + a], 0:CHUNKS * GS].rearrange("p (c g) -> p c g", c=CHUNKS),
                        ACT.Copy).then_inc(slots_kept, 1)

            keep_slots(0)
            keep_slots(1)
            split(0, range(UNITS // 2))
            split(0, range(UNITS // 2, UNITS))
            act.wait_ge(consts_made, 3)
            act.wait_ge(flag_set, 1)
            fast = act.value_load(flag[0:1, 0:1], min_val=0, max_val=1)
            with act.If(fast == 1):
                def keep_count(g, s, q):
                    act.wait_ge(counted, g + (q + 1 + RING))
                    nc.scalar.activation(stage[:, s, q % GT, :], PS[:, COUNT_BANKS[q % 2], 0:RB], ACT.Copy).then_inc(count_kept, 1)

                act.sem_inc(count_kept, 2)
                act.sem_inc(stored[0], 16 * RANGES)
                act.sem_inc(stored[1], 16 * RANGES)
                with act.Fori(0, (KT - 1) // 2) as i:
                    for s in range(2):
                        act.wait_ge(stored[s], i * (16 * RANGES) + 16 * RANGES)
                        for q in range(s * GT, (s + 1) * GT):
                            keep_count(i * (2 * GT), s, q)
                act.wait_ge(stored[0], 16 * RANGES * ((KT - 1) // 2 + 1))
                for q in range(GLAST):
                    keep_count((KT - 1) * GT, 0, q)
                act.wait_ge(stored[0], 16 * RANGES * ((KT - 1) // 2 + 2))
                act.wait_ge(stored[1], 16 * RANGES * ((KT - 1) // 2 + 1))
                for j in range(BLOCKS + 1):
                    lo, hi = j * BANK, min((j + 1) * BANK, NP)
                    act.wait_ge(first_made, j + 1)
                    nc.scalar.activation(agg[:, lo:hi], PS[:, j, 0:hi - lo],
                                         ACT.Copy).then_inc(agg_kept, 1 if j < BLOCKS else RANGES - BLOCKS)
                act.sem_inc(rz_ready, 1)
                act.sem_inc(h_ready, RANGES)

                def keep_agg(t, b):
                    act.wait_ge(agg_made, (t - 1) * RANGES + (b + 1))
                    nc.scalar.activation(agg[:, b * RB:(b + 1) * RB], PS[:, AGG_BANKS[b % 2], 0:RB],
                                         ACT.Copy).then_inc(agg_kept, 1)

                def gate_functions(t, b, seconds=(), firsts=()):
                    c = t * RANGES
                    act.wait_ge(rz_made, c + (b + 1))
                    act.wait_ge(pre_ready, c + (b + 1))
                    act.wait_ge(h_ready, c + (RANGES + b - 1))
                    nc.scalar.activation(gate_r, PS[:, R_BANK, 0:RB], ACT.Sigmoid, bias=brz[:, 0:1])
                    nc.scalar.activation(gate_z[b % 2], PS[:, Z_BANK, 0:RB], ACT.Sigmoid, bias=brz[:, 1:2]).then_inc(rz_ready, 1)
                    for u in seconds:
                        part(t + 1, u, 1)
                    act.wait_ge(pre_ready, c + (b + 2))
                    nc.scalar.activation(cand, pre_n, ACT.Tanh, bias=bih[:, 2:3]).then_inc(cand_ready, 1)
                    for u in firsts:
                        part(t + 1, u, 0)

                for b in range(RANGES):
                    gate_functions(0, b, first_units(b - 1), first_units(b))
                for u in first_units(RANGES - 1):
                    part(1, u, 1)

                def step(t, last):
                    split(t, range(EARLY, LATE))
                    split(t, range(LATE, UNITS))
                    for b in range(RANGES):
                        keep_agg(t, b)
                        if b == RANGES - 2 and not last:
                            split(t + 1, range(MIDDLE))
                        gate_functions(t, b)
                        if b == RANGES - 2 and not last:
                            split(t + 1, range(MIDDLE, EARLY))
                        if b == RANGES - 2 and last:
                            deviation(0, EARLY_QUADS)
                    if last:
                        deviation(EARLY_QUADS, QUADS)

                with act.Fori(1, STEPS - 1) as t:
                    step(t, last=False)
                step(STEPS - 1, last=True)
            with act.Else():
                act.sem_inc(h_ready, RANGES)
                with act.Fori(0, STEPS) as t:
                    act.wait_ge(gs_summed, t + 1)
                    last = nc.scalar.activation(g_agg.rearrange("p (r c) -> p r c", r=RANGES), PS[:, :, 0:RB], ACT.Copy)
                    last.then_inc(gs_agg_kept, 1)
                    for b in range(RANGES):
                        act.wait_ge(gs_gates_made, t * RANGES + (b + 1))
                        nc.scalar.activation(gate_r, PS[:, 2, 0:RB], ACT.Sigmoid, bias=brz[:, 0:1])
                        nc.scalar.activation(gate_z[0], PS[:, 3, 0:RB], ACT.Sigmoid, bias=brz[:, 1:2]).then_inc(gs_rz_ready, 1)
                        act.wait_ge(gs_pre_ready, t * RANGES + (b + 1))
                        nc.scalar.activation(cand, pre_n, ACT.Tanh, bias=bih[:, 2:3]).then_inc(gs_cand_ready, 1)
                deviation(0, QUADS)

        @block.vector
        def _(dve):
            order = [0]

            def link(ins):
                order[0] += 1
                ins.then_inc(prep_chain, 1)
                dve.wait_ge(prep_chain, order[0])

            dve.wait_ge(dst_in, 16)
            link(nc.vector.tensor_copy(first_dst, dst_rows[0:DR, 0:1]))

            def message(t, u):
                w = width(u)
                dve.wait_ge(msg_made, t * UNITS + (u + 1))
                dve.wait_ge(rest_done, t * UNITS + (u + 1))
                nc.vector.tensor_tensor(msg32[u % 2][:, 0:w, :],
                                        PS[:, MSG_BANKS[u % 2], 0:w * H].rearrange("p (k h) -> p k h", k=w),
                                        bmsg[:, :].unsqueeze(1).to_broadcast([P, w, H]),
                                        ALU.add).then_inc(msg32_ready, 1)

            def leave(t, u):
                w = width(u)
                dve.wait_ge(part1_done, t * UNITS + (u + 1))
                dve.wait_ge(parts_ready, t * UNITS + (u + 1))
                nc.vector.tensor_tensor(rest[u % 2][:, 0:w, :], msg32[u % 2][:, 0:w, :],
                                        parts[:, 2 * u:2 * u + w, 0, :], ALU.subtract).then_inc(rest_done, 1)

            def messages(t, units):
                for u in units:
                    if u == units[0]:
                        message(t, u)
                    if u < units[-1]:
                        message(t, u + 1)
                    leave(t, u)

            def statistics(g):
                tiles, n = quad(g)
                a, z = tiles[0], tiles[-1] + 1
                dve.wait_ge(x2_in, 16 * MOVES)
                dve.wait_ge(out_turned, g + 1)
                nc.vector.tensor_tensor(y[0:n, a:z, :], y[0:n, a:z, :],
                                        PS[0:n, MSG_BANKS[g % 2], 0:(z - a) * P].rearrange("p (k h) -> p k h", h=P),
                                        ALU.add).then_inc(y_made, 1)
                dve.wait_ge(y_made, g + 1)
                for k in tiles:
                    last = nc.vector.bn_stats(stats[0:n, k, :], y[0:n, k, :])
                last.then_inc(stats_made, 1)
                dve.wait_ge(stats_made, g + 1)
                for k in tiles:
                    nc.vector.bn_aggr(mv[0:n, k, :], stats[0:n, k, :]).then_inc(mv_made, 1)

            def norm(first, past):
                for g in range(first, past):
                    tiles, n = quad(g)
                    a, z = tiles[0], tiles[-1] + 1
                    dve.wait_ge(std_made, g + 1)
                    nc.vector.reciprocal(rstd[0:n, a:z, 0], std[0:n, a:z, 0]).then_inc(rstd_made, 1)
                dve.wait_ge(rstd_made, past)
                for g in range(first, past):
                    tiles, n = quad(g)
                    for k in tiles:
                        nc.vector.tensor_scalar(res[0:n, k, :], y[0:n, k, :], mv[0:n, k, 0:1], rstd[0:n, k, 0:1],
                                                ALU.subtract, ALU.mult).then_inc(res_made, 1)

            dve.sem_inc(msg32_ready, 2)
            dve.sem_inc(parts_ready, 2)
            dve.sem_inc(rest_done, 2)
            dve.wait_ge(consts_made, 1)
            nc.vector.tensor_scalar(below[0:DR, :], thr_row[0:DR, :], first_dst, None, ALU.is_gt).then_inc(below_made, 1)
            dve.wait_ge(rows_counted, 1)
            link(nc.vector.tensor_scalar(row_f, PS[0:GS, 0, 0:SETS], -1.0, 0.0, ALU.add, ALU.max))
            nc.vector.tensor_copy(row_i, row_f).then_inc(rows_set, 1)
            dve.wait_ge(b_in, 48)
            nc.vector.tensor_tensor(brz[:, :], bih[:, 0:2], bhh[:, 0:2], ALU.add)
            dve.wait_ge(rows_in, 32)
            for s in range(SETS):
                last = nc.vector.tensor_scalar(key[0:GS, :, :].rearrange("p s w -> p (s w)")[:, 0:DW], row_of[0:GS, s, :],
                                               thr_part[:, s:s + 1], 0.0, ALU.is_lt, ALU.add,
                                               accum_out=before[:, s:s + 1])
                link(last)
            link(nc.vector.scalar_tensor_tensor(out=start_f, in0=row_f, scalar=float(DW), in1=before,
                                                op0=ALU.mult, op1=ALU.add))
            nc.vector.tensor_scalar(start_i, start_f, float(E - WIN), None, ALU.min).then_inc(starts_set, 1)
            for s in range(SETS):
                v2 = rng[0:GS, s, :]
                d, r, k, v, a, w = (t[0:GS, s, :] for t in (win_dst, win_src, key, valid, rng, rowin))
                r2, r3 = place_c[0:GS, :], place_q[0:GS, :]
                dve.wait_ge(windows_in[s], 32)
                link(nc.vector.tensor_scalar(k, d, thr_part[:, s:s + 1], None, ALU.subtract))
                link(nc.vector.tensor_scalar(v, k, 0.0, None, ALU.is_ge))
                link(nc.vector.scalar_tensor_tensor(out=v, in0=k, scalar=float(GROUP), in1=v, op0=ALU.is_lt,
                                                    op1=ALU.mult, accum_out=matched[:, s:s + 1]))
                link(nc.vector.tensor_scalar(r2, r, GROUP - 1, None, ALU.bitwise_and))
                link(nc.vector.tensor_scalar(r3, r, 4, GT - 1, ALU.logical_shift_right, ALU.bitwise_and))
                link(nc.vector.scalar_tensor_tensor(out=w, in0=r2, scalar=float(GT - 1), in1=r, op0=ALU.mult, op1=ALU.add))
                link(nc.vector.scalar_tensor_tensor(out=w, in0=r3, scalar=-float(GROUP - 1), in1=w, op0=ALU.mult,
                                                    op1=ALU.add))
                link(nc.vector.scalar_tensor_tensor(out=v2, in0=r, scalar=float((KT - 1) * P), in1=r2, op0=ALU.is_ge,
                                                    op1=ALU.mult))
                link(nc.vector.scalar_tensor_tensor(out=w, in0=v2, scalar=-float(GT - GLAST), in1=w, op0=ALU.mult,
                                                    op1=ALU.add))
                link(nc.vector.tensor_scalar(a, w, -(RB - 1) / 2, 1.0 / RB, ALU.add, ALU.mult))
                link(nc.vector.tensor_scalar(a, a, ROUND, None, ALU.add))
                link(nc.vector.tensor_scalar(a, a, ROUND, None, ALU.subtract))
                link(nc.vector.scalar_tensor_tensor(out=w, in0=a, scalar=-float(RB), in1=w, op0=ALU.mult, op1=ALU.add))
                link(nc.vector.scalar_tensor_tensor(out=k, in0=a, scalar=float(GROUP), in1=k, op0=ALU.mult, op1=ALU.add))
                last = nc.vector.scalar_tensor_tensor(out=k, in0=k, scalar=1.0, in1=v, op0=ALU.add, op1=ALU.mult)
                last.then_inc(keys_made, 1)
                dve.wait_ge(keys_made, s + 1)
            nc.vector.tensor_copy(matched, matched).then_inc(matched_made, 1)
            messages(0, range(UNITS // 2))
            dve.wait_ge(matched_summed, 1)
            nc.vector.tensor_scalar(flag[0:1, 0:1], PS[0:1, 7, 0:1], float(E), None, ALU.is_equal).then_inc(flag_set, 1)
            messages(0, range(UNITS // 2, UNITS))
            dve.wait_ge(parts_ready, UNITS + 2)
            dve.wait_ge(slots_kept, 2 * SETS)
            dve.wait_ge(x_kept, -(-KT // 4))
            dve.wait_ge(consts_made, 3)
            dve.wait_ge(flag_set, 1)
            fast = dve.value_load(flag[0:1, 0:1], min_val=0, max_val=1)
            with dve.If(fast == 1):
                def one_hots(g, q):
                    dve.wait_ge(counted, g + (q + (2 if q % PAIR == 0 else 1)))
                    if q % PAIR == 0:
                        nc.vector.tensor_tensor(
                            hot_key[:, q // PAIR % 2, :, :], iota_key.rearrange("p (m c) -> p m c", m=P),
                            keyT[:, bass.ds((g + q) * CHUNKS, PAIR * CHUNKS)].unsqueeze(1).to_broadcast(
                                [P, P, PAIR * CHUNKS]), ALU.is_equal)
                    for c in range(CHUNKS):
                        last = nc.vector.tensor_scalar(hot_row[q % RING][:, c, :], iota_row,
                                                       rowT[:, bass.ds((g + q) * CHUNKS + c, 1)], None, ALU.is_equal)
                    last.then_inc(hots_ready, 1)

                dve.sem_inc(counted, RING)
                with dve.Fori(0, (KT - 1) // 2) as i:
                    for q in range(2 * GT):
                        one_hots(i * (2 * GT), q)
                for q in range(GLAST):
                    one_hots((KT - 1) * GT, q)
                dve.sem_inc(pre_ready, 1)

                def update(t, b, units=()):
                    c = t * RANGES
                    hb = hT[:, b * RB:(b + 1) * RB]
                    dve.wait_ge(n_made, c + (b + 1))
                    dve.wait_ge(rz_ready, c + (b + 2))
                    nc.vector.scalar_tensor_tensor(out=pre_n, in0=PS[:, HN_BANK, 0:RB], scalar=bhh[:, 2:3], in1=gate_r,
                                                   op0=ALU.add, op1=ALU.mult).then_inc(n_half, 1)
                    dve.wait_ge(n_half, c + (b + 1))
                    nc.vector.tensor_tensor(pre_n, PS[:, IN_BANK, 0:RB], pre_n, ALU.add).then_inc(pre_ready, 1)
                    for u in units:
                        message(t + 1, u)
                    dve.wait_ge(cand_ready, c + (b + 1))
                    nc.vector.tensor_tensor(diff, hb, cand, ALU.subtract).then_inc(d_made, 1)
                    dve.wait_ge(d_made, c + (b + 1))
                    nc.vector.tensor_tensor(diff, gate_z[b % 2], diff, ALU.mult).then_inc(zd_made, 1)
                    dve.wait_ge(zd_made, c + (b + 1))
                    nc.vector.tensor_tensor(hb, cand, diff, ALU.add).then_inc(h_ready, 1)
                    for u in units:
                        leave(t + 1, u)

                for b in range(RANGES):
                    update(0, b, first_units(b))

                def step(t, last):
                    messages(t, range(EARLY, LATE))
                    messages(t, range(LATE, UNITS))
                    for b in range(RANGES):
                        if b == RANGES - 2 and not last:
                            messages(t + 1, range(MIDDLE))
                        if last:
                            for g in range(EARLY_QUADS):
                                if quad_ranges(g) == b:
                                    statistics(g)
                        if b == RANGES - 1 and last:
                            norm(0, EARLY_QUADS)
                            statistics(EARLY_QUADS)
                        update(t, b)
                        if b == RANGES - 2 and not last:
                            messages(t + 1, range(MIDDLE, EARLY))
                    if last:
                        statistics(QUADS - 2)
                        statistics(QUADS - 1)
                        norm(EARLY_QUADS, QUADS)

                with dve.Fori(1, STEPS - 1) as t:
                    step(t, last=False)
                step(STEPS - 1, last=True)
            with dve.Else():
                dve.wait_ge(gs_src_in, 16)
                nc.vector.tensor_scalar(g_c[0:DR, :], g_src[0:DR, :], GROUP - 1, None, ALU.bitwise_and)
                nc.vector.tensor_scalar(g_q[0:DR, :], g_src[0:DR, :], 4, GT - 1, ALU.logical_shift_right,
                                        ALU.bitwise_and).then_inc(gs_rows, 1)
                dve.wait_ge(gs_rows, 1)
                nc.vector.scalar_tensor_tensor(out=g_row[0:DR, :], in0=g_c[0:DR, :], scalar=float(GT - 1),
                                               in1=g_src[0:DR, :], op0=ALU.mult, op1=ALU.add).then_inc(gs_rows, 1)
                dve.wait_ge(gs_rows, 2)
                nc.vector.scalar_tensor_tensor(out=g_row[0:DR, :], in0=g_q[0:DR, :], scalar=-float(GROUP - 1),
                                               in1=g_row[0:DR, :], op0=ALU.mult, op1=ALU.add).then_inc(gs_rows, 1)
                nc.vector.scalar_tensor_tensor(out=g_last[0:DR, :], in0=g_src[0:DR, :], scalar=float((KT - 1) * P),
                                               in1=g_c[0:DR, :], op0=ALU.is_ge, op1=ALU.mult).then_inc(gs_rows, 1)
                dve.wait_ge(gs_rows, 4)
                nc.vector.scalar_tensor_tensor(out=g_row[0:DR, :], in0=g_last[0:DR, :], scalar=-float(GT - GLAST),
                                               in1=g_row[0:DR, :], op0=ALU.mult, op1=ALU.add).then_inc(gs_rows, 1)
                dve.wait_ge(gs_rows, 5)
                dve.wait_ge(gs_consts, 1)
                dve.sem_inc(gs_used, 1)
                dve.sem_inc(gs_msg_kept, 1)
                dve.sem_inc(gs_msg_stored, 16)
                with dve.Fori(0, STEPS) as t:
                    for u in range(MU):
                        w = min(4, KT - 4 * u)
                        dve.wait_ge(gs_msg_made, t * MU + (u + 1))
                        if u == 0:
                            dve.wait_ge(gs_msg_stored, t * (16 * MOVES) + 16)
                        n = KLAST if w == 1 else P
                        nc.vector.tensor_tensor(g_msg[0:n, 4 * u:4 * u + w, :],
                                                PS[0:n, 0, 0:w * H].rearrange("p (k h) -> p k h", k=w),
                                                bmsg[0:n, :].unsqueeze(1).to_broadcast([n, w, H]),
                                                ALU.add).then_inc(gs_msg_kept, 1)
                    with dve.Fori(0, DW) as e:
                        dve.wait_ge(gs_used, t * DW + (e + 1))
                        nc.vector.tensor_copy(g_index[0:DR, :], dst_rows[0:DR, bass.ds(e, 1)]).then_inc(gs_index, 1)
                        nc.vector.tensor_scalar(g_hot[0:DR, :], g_iota[0:DR, :], g_row[0:DR, bass.ds(e, 1)], None,
                                                ALU.is_equal).then_inc(gs_hot, 1)
                    for b in range(RANGES):
                        c = t * RANGES
                        hb = hT[:, b * RB:(b + 1) * RB]
                        dve.wait_ge(gs_rz_ready, c + (b + 1))
                        nc.vector.scalar_tensor_tensor(out=pre_n, in0=PS[:, 4, 0:RB], scalar=bhh[:, 2:3], in1=gate_r,
                                                       op0=ALU.add, op1=ALU.mult).then_inc(gs_half, 1)
                        dve.wait_ge(gs_half, c + (b + 1))
                        nc.vector.tensor_tensor(pre_n, PS[:, 5, 0:RB], pre_n, ALU.add).then_inc(gs_pre_ready, 1)
                        dve.wait_ge(gs_cand_ready, c + (b + 1))
                        nc.vector.tensor_tensor(diff, hb, cand, ALU.subtract).then_inc(gs_d_made, 1)
                        dve.wait_ge(gs_d_made, c + (b + 1))
                        nc.vector.tensor_tensor(diff, gate_z[0], diff, ALU.mult).then_inc(gs_zd_made, 1)
                        dve.wait_ge(gs_zd_made, c + (b + 1))
                        nc.vector.tensor_tensor(hb, cand, diff, ALU.add).then_inc(h_ready, 1)
                for g in range(QUADS):
                    statistics(g)
                norm(0, QUADS)


_INS = ['x', 'src', 'dst', 'L0_gnn_W_msg', 'L0_gnn_b_msg', 'L0_gnn_W_ih', 'L0_gnn_W_hh', 'L0_gnn_b_ih', 'L0_gnn_b_hh']


def kernel(**inputs):
    import numpy as _np
    import concourse.bacc as _bacc
    from concourse import mybir as _mybir
    from concourse.bass_utils import run_bass_kernel_spmd as _run

    nc = _bacc.Bacc("TRN2", target_bir_lowering=False, num_devices=1, dynamic_dma_scratch_size=8192)
    arrays, args = {}, []
    for name in _INS:
        a = _np.ascontiguousarray(inputs[name])
        arrays[f"in_{name}"] = a
        args.append(nc.dram_tensor(f"in_{name}", a.shape, _mybir.dt.from_np(a.dtype), kind="ExternalInput").ap())
    args.append(nc.dram_tensor("out", inputs['x'].shape, _mybir.dt.float32, kind="ExternalOutput").ap())
    gnn_kernel(nc, *args)
    r = _run(nc, [arrays], core_ids=[0])
    return r.results[0]["out"]
```
